# Optimizing a Trainium2 kernel written in Bass

```python
import numpy as np
import jax
import jax.numpy as jnp

def _softmax(x, axis=-1):
    return jax.nn.softmax(x, axis=axis)

def _gelu(x):
    return jax.nn.gelu(x, approximate=True)

def _silu(x):
    return jax.nn.silu(x)

def _sigmoid(x):
    return jax.nn.sigmoid(x)

def _layernorm(x, axis=-1, eps=1e-05):
    m = jnp.mean(x, axis=axis, keepdims=True)
    v = jnp.var(x, axis=axis, keepdims=True)
    return (x - m) / jnp.sqrt(v + eps)

def _scatter_add(tgt, idx, src, axis=0):
    return tgt.at[idx].add(src)

def _segment_sum(src, seg, n):
    return jax.ops.segment_sum(src, seg, n)
kernel_name = 'mk_seq_preln_d1_jaxref_r4_48b1ac'

def setup_inputs(seed: int=0):
    np.random.seed(seed)
    _w = jnp.asarray

    def _L0_attn_setup():
        import jax, jax.numpy as jnp
        import numpy as np
        B, N, D, H = (4, 1024, 256, 16)
        HD = D // H
        MLP = 4 * D

        def _ln(x, w, b):
            m = x.mean(-1, keepdims=True)
            v = x.var(-1, keepdims=True)
            return (x - m) / jnp.sqrt(v + 1e-05) * w + b
        key = jax.random.key(seed)
        ks = jax.random.split(key, 12)
        s = 1.0 / np.sqrt(D)
        sm = 1.0 / np.sqrt(MLP)
        return {'q_x': jax.random.normal(ks[0], (B, N, D), jnp.float32), 'ln1_w': jnp.ones((D,), jnp.float32), 'ln1_b': jnp.zeros((D,), jnp.float32), 'wq': jax.random.normal(ks[1], (D, D), jnp.float32) * s, 'bq': jnp.zeros((D,), jnp.float32), 'wk': jax.random.normal(ks[2], (D, D), jnp.float32) * s, 'bk': jnp.zeros((D,), jnp.float32), 'wv': jax.random.normal(ks[3], (D, D), jnp.float32) * s, 'bv': jnp.zeros((D,), jnp.float32), 'wo': jax.random.normal(ks[4], (D, D), jnp.float32) * s, 'bo': jnp.zeros((D,), jnp.float32), 'ln2_w': jnp.ones((D,), jnp.float32), 'ln2_b': jnp.zeros((D,), jnp.float32), 'fc_w': jax.random.normal(ks[5], (D, MLP), jnp.float32) * s, 'fc_b': jnp.zeros((MLP,), jnp.float32), 'proj_w': jax.random.normal(ks[6], (MLP, D), jnp.float32) * sm, 'proj_b': jnp.zeros((D,), jnp.float32)}
    _L0_attn_in = _L0_attn_setup()

    def _L0_ffn_setup():
        import jax, jax.numpy as jnp
        import numpy as np
        B, T, D = (4, 1024, 256)
        E = 8
        TOP_K = 2
        FFN = 768
        HALF = FFN // 2

        def _kaiming_uniform(key, shape, fan_in):
            bound = 1.0 / np.sqrt(fan_in)
            return jax.random.uniform(key, shape, jnp.float32, -bound, bound)
        key = jax.random.key(seed)
        ks = jax.random.split(key, 7)
        x = jax.random.normal(ks[0], (B, T, D), jnp.float32)
        gate_w = _kaiming_uniform(ks[1], (E, D), D) * 0.01
        w_up = _kaiming_uniform(ks[2], (E, FFN, D), D)
        w_down = _kaiming_uniform(ks[3], (E, D, HALF), HALF)
        sg_gate = _kaiming_uniform(ks[4], (HALF, D), D)
        sg_up = _kaiming_uniform(ks[5], (HALF, D), D)
        sg_down = _kaiming_uniform(ks[6], (D, HALF), HALF)
        return {'x': x, 'gate_w': gate_w, 'w_up': w_up, 'w_down': w_down, 'sg_gate': sg_gate, 'sg_up': sg_up, 'sg_down': sg_down}
    _L0_ffn_in = _L0_ffn_setup()
    _d = {'L0_attn_q_x': _L0_attn_in['q_x'], 'L0_attn_ln1_w': _L0_attn_in['ln1_w'], 'L0_attn_ln1_b': _L0_attn_in['ln1_b'], 'L0_attn_wq': _L0_attn_in['wq'], 'L0_attn_bq': _L0_attn_in['bq'], 'L0_attn_wk': _L0_attn_in['wk'], 'L0_attn_bk': _L0_attn_in['bk'], 'L0_attn_wv': _L0_attn_in['wv'], 'L0_attn_bv': _L0_attn_in['bv'], 'L0_attn_wo': _L0_attn_in['wo'], 'L0_attn_bo': _L0_attn_in['bo'], 'L0_attn_ln2_w': _L0_attn_in['ln2_w'], 'L0_attn_ln2_b': _L0_attn_in['ln2_b'], 'L0_attn_fc_w': _L0_attn_in['fc_w'], 'L0_attn_fc_b': _L0_attn_in['fc_b'], 'L0_attn_proj_w': _L0_attn_in['proj_w'], 'L0_attn_proj_b': _L0_attn_in['proj_b'], 'L0_ffn_gate_w': _L0_ffn_in['gate_w'], 'L0_ffn_w_up': _L0_ffn_in['w_up'], 'L0_ffn_w_down': _L0_ffn_in['w_down'], 'L0_ffn_sg_gate': _L0_ffn_in['sg_gate'], 'L0_ffn_sg_up': _L0_ffn_in['sg_up'], 'L0_ffn_sg_down': _L0_ffn_in['sg_down']}
    _x0 = _d['L0_attn_q_x']
    _d['L0_attn_q_x'] = jax.random.normal(jax.random.fold_in(jax.random.key(seed), 1), (16, 512, 256), dtype=_x0.dtype)
    del _x0
    return _d

def reference(L0_attn_q_x, L0_attn_ln1_w, L0_attn_ln1_b, L0_attn_wq, L0_attn_bq, L0_attn_wk, L0_attn_bk, L0_attn_wv, L0_attn_bv, L0_attn_wo, L0_attn_bo, L0_attn_ln2_w, L0_attn_ln2_b, L0_attn_fc_w, L0_attn_fc_b, L0_attn_proj_w, L0_attn_proj_b, L0_ffn_gate_w, L0_ffn_w_up, L0_ffn_w_down, L0_ffn_sg_gate, L0_ffn_sg_up, L0_ffn_sg_down):

    def _L0_attn_ref(q_x, ln1_w, ln1_b, wq, bq, wk, bk, wv, bv, wo, bo, ln2_w, ln2_b, fc_w, fc_b, proj_w, proj_b):
        import jax, jax.numpy as jnp
        import numpy as np
        B, N, D, H = (4, 1024, 256, 16)
        HD = D // H
        MLP = 4 * D

        def _ln(x, w, b):
            m = x.mean(-1, keepdims=True)
            v = x.var(-1, keepdims=True)
            return (x - m) / jnp.sqrt(v + 1e-05) * w + b
        b, n, c = q_x.shape
        xn = _ln(q_x, ln1_w, ln1_b)
        q = (xn @ wq + bq).reshape(b, n, H, HD).transpose(0, 2, 1, 3)
        k = (xn @ wk + bk).reshape(b, n, H, HD).transpose(0, 2, 1, 3)
        v = (xn @ wv + bv).reshape(b, n, H, HD).transpose(0, 2, 1, 3)
        fq = jax.nn.elu(q) + 1.0
        fk = jax.nn.elu(k) + 1.0
        kv = jnp.einsum('bhnd,bhne->bnde', fk, v)
        qkv = jnp.einsum('bhnd,bnde->bhne', fq, kv)
        k_sum = fk.sum(axis=1)
        qk = jnp.einsum('bhnd,bnd->bhn', fq, k_sum)
        attn = qkv / (qk[..., None] + 1e-06)
        attn = attn.transpose(0, 2, 1, 3).reshape(b, n, c)
        attn = attn @ wo + bo
        x = q_x + attn
        h = _ln(x, ln2_w, ln2_b)
        h = jax.nn.gelu(h @ fc_w + fc_b, approximate=False)
        return x + (h @ proj_w + proj_b)

    def _L0_ffn_ref(x, gate_w, w_up, w_down, sg_gate, sg_up, sg_down):
        import jax, jax.numpy as jnp
        import numpy as np
        B, T, D = (4, 1024, 256)
        E = 8
        TOP_K = 2
        FFN = 768
        HALF = FFN // 2

        def _kaiming_uniform(key, shape, fan_in):
            bound = 1.0 / np.sqrt(fan_in)
            return jax.random.uniform(key, shape, jnp.float32, -bound, bound)
        b, t, d = x.shape
        xf = x.reshape(b * t, d)
        N = xf.shape[0]
        logits = xf @ gate_w.T
        topk_logits, topk_idx = jax.lax.top_k(logits, TOP_K)
        topk_w = jax.nn.softmax(topk_logits.astype(jnp.float32), axis=-1).astype(x.dtype)
        comb = jnp.zeros((N, E), x.dtype).at[jnp.arange(N)[:, None], topk_idx].add(topk_w)
        wg = w_up[:, :HALF, :]
        wu = w_up[:, HALF:, :]
        out = jnp.zeros_like(xf)
        for e in range(E):
            g = xf @ wg[e].T
            u = xf @ wu[e].T
            y = jax.nn.silu(g) * u @ w_down[e].T
            out = out + comb[:, e:e + 1] * y
        shared = jax.nn.silu(xf @ sg_gate.T) * (xf @ sg_up.T) @ sg_down.T
        return (shared + out).reshape(b, t, d)
    x = L0_attn_q_x
    x = x + _L0_attn_ref(_layernorm(x, axis=-1), L0_attn_ln1_w, L0_attn_ln1_b, L0_attn_wq, L0_attn_bq, L0_attn_wk, L0_attn_bk, L0_attn_wv, L0_attn_bv, L0_attn_wo, L0_attn_bo, L0_attn_ln2_w, L0_attn_ln2_b, L0_attn_fc_w, L0_attn_fc_b, L0_attn_proj_w, L0_attn_proj_b)
    x = x + _L0_ffn_ref(_layernorm(x, axis=-1), L0_ffn_gate_w, L0_ffn_w_up, L0_ffn_w_down, L0_ffn_sg_gate, L0_ffn_sg_up, L0_ffn_sg_down)
    return x

_drawn_inputs = setup_inputs


def setup_inputs(seed=0):
    import zlib

    import numpy as np

    out = dict(_drawn_inputs(seed))
    spreads = {'L0_attn_ln1_w': (1.0, 0.2),
     'L0_attn_ln1_b': (0.0, 0.652),
     'L0_attn_bq': (0.0, 0.8),
     'L0_attn_bk': (0.0, 0.8),
     'L0_attn_bv': (0.0, 0.565),
     'L0_attn_bo': (0.0, 0.1),
     'L0_attn_ln2_w': (1.0, 0.2),
     'L0_attn_ln2_b': (0.0, 0.1),
     'L0_attn_fc_b': (0.0, 0.1),
     'L0_attn_proj_b': (0.0, 0.1)}
    factors = {'L0_attn_wq': 3.189}
    for name, (base, spread) in spreads.items():
        noise = np.random.default_rng([zlib.crc32(name.encode()), seed]).standard_normal(out[name].shape)
        drawn = base * np.exp(spread * noise) if base else spread * noise
        out[name] = jnp.asarray(drawn.astype(out[name].dtype))
    for name, factor in factors.items():
        out[name] = (out[name] * factor).astype(out[name].dtype)
    return out
```

```python
from contextlib import ExitStack

import concourse.bass as bass
from concourse import mybir

FP32 = mybir.dt.float32
BF16 = mybir.dt.bfloat16
INT32 = mybir.dt.int32
UINT32 = mybir.dt.uint32
ALU = mybir.AluOpType
ACT = mybir.ActivationFunctionType
AX = mybir.AxisListType

P = 128
TOKENS = 16 * 512
D = 256
KC = D // P
HEADS = 16
HD = D // HEADS
MLP = 4 * D
FCH = MLP // P
EXPERTS = 8
HALF = 384
HCH = HALF // P
TPB = 4
BLOCK = TPB * P
BLOCKS = TOKENS // BLOCK
EPS = 1e-5

REGION = TOKENS + P
SORTED_TILES = 2 * TOKENS // P + EXPERTS
SPARE_TILES = EXPERTS
ROW = D + 4
C_TOK, C_W0, C_W1, C_E0 = D, D + 1, D + 2, D + 3
EXW = KC * 2 * HALF + HCH * D

POOL_TILE = 3
ORDER = (POOL_TILE, 0, 1, 2)
POOL_STEPS, DVE_STEPS = 8, 95
HE = HD + 1


def build(nc, x, wqkv, b_tok, ln1w, ln1b, ln2w, ln2b, wo, fc_w, fc_b, proj_w, gate_w, sg_up, sg_down,
          experts, out):
    ctx = ExitStack()
    with ctx:
        def sb(name, shape, dt=FP32):
            return ctx.enter_context(nc.sbuf_tensor(name, shape, dt))

        def sem(name):
            return ctx.enter_context(nc.semaphore(name))

        x_blk = x.rearrange("(b t p) d -> b p t d", t=TPB, p=P)
        out_blk = out[0:TOKENS, :].rearrange("(b t p) d -> b p t d", t=TPB, p=P)
        rows_sorted = nc.dram_tensor("rows_sorted", [EXPERTS * REGION + SPARE_TILES * P, ROW], FP32,
                                     kind="Internal").ap()

        wqkv_sb = sb("wqkv_sb", [P, KC, 3 * D])
        wo_sb = sb("wo_sb", [P, KC, D])
        fc_sb = sb("fc_sb", [P, KC, MLP])
        proj_sb = sb("proj_sb", [P, FCH, D])
        gate_sb = sb("gate_sb", [P, KC, EXPERTS])
        sgup_sb = sb("sgup_sb", [P, KC, 2 * HALF])
        sgdn_sb = sb("sgdn_sb", [P, HCH, D])
        exp_sb = sb("exp_sb", [P, EXPERTS, EXW])
        ln_sb = sb("ln_sb", [P, 4, KC])
        fcb_sb = sb("fcb_sb", [P, FCH])
        ones_bf = sb("ones_bf", [P, P], BF16)
        before_bf = sb("before_bf", [P, P], BF16)
        bias_bf = sb("bias_bf", [P, 5 * D], BF16)
        ident = sb("ident", [P, P])

        xin = sb("xin", [P, TPB, D])
        xnT = [sb(f"xnT{j}", [P, KC, P]) for j in range(2)]
        eqk = sb("eqk", [P, 2 * D])
        rqk = sb("rqk", [P, 2 * D])
        v_dve = [sb(f"v_dve{j}", [P, HD, HEADS]) for j in range(2)]
        v_pool = sb("v_pool", [P, HEADS, HE])
        fq = sb("fq", [P, HEADS, HD])
        fqk_pool = sb("fqk_pool", [P, 2, HEADS, HD])
        prod = sb("prod", [P, HEADS * HE * HD])
        prod_pool = sb("prod_pool", [P, HEADS * HE * HD])
        qkv = sb("qkv", [P, HEADS, HE])
        kv_pool = sb("kv_pool", [P, HD, HE])
        qkv_pool = sb("qkv_pool", [P, HEADS, HE])
        attn = sb("attn", [P, TPB, D])
        xres = sb("xres", [P, TPB, D])
        xmid = sb("xmid", [P, TPB, D])
        bT = sb("bT", [P, KC, BLOCK])
        hid = sb("hid", [P, FCH, BLOCK])
        x1 = sb("x1", [P, TPB, D])
        rows = sb("rows", [P, TPB, ROW])
        sg_g = hid[:, 0:HCH, :]
        sg_u = hid[:, HCH:2 * HCH, :]
        st6 = sb("st6", [P, TPB, 6])
        mv_a = sb("mv_a", [P, TPB, 2])
        sq_a = sb("sq_a", [P, 2, TPB])
        rs_a = sb("rs_a", [P, 2, TPB])
        a_scale = sb("a_scale", [P, 2, TPB])
        mv_b = sb("mv_b", [P, TPB, 2])
        sq_b = sb("sq_b", [P, TPB])
        rs_b = sb("rs_b", [P, TPB])
        den = sb("den", [P, HEADS])
        logit = sb("logit", [P, TPB, EXPERTS])
        top_v = sb("top_v", [P, TPB, 8])
        top_i = sb("top_i", [P, TPB, 8], UINT32)
        iota_e = sb("iota_e", [P, EXPERTS])
        iota_r = sb("iota_r", [P, EXPERTS])
        first2 = sb("first2", [P, 2, TPB])
        gap = sb("gap", [P, TPB])
        gap_e = sb("gap_e", [P, TPB])
        onehot = sb("onehot", [P, 2, TPB, EXPERTS])
        chosen = sb("chosen", [P, TPB, EXPERTS], BF16)
        free_row = sb("free_row", [P, EXPERTS])
        rank = sb("rank", [P, TPB, EXPERTS])
        slot_w = sb("slot_w", [P, 2, TPB, EXPERTS])
        slot = sb("slot", [P, 2 * TPB], INT32)
        tok = sb("tok", [P, TPB])
        pad_row = sb("pad_row", [P, ROW])
        pad_at = sb("pad_at", [P, EXPERTS], INT32)
        iota_p = sb("iota_p", [P, 1])
        cnt_i = sb("cnt_i", [P, EXPERTS], INT32)
        tiles_f = sb("tiles_f", [P, EXPERTS])
        tiles_to = sb("tiles_to", [P, EXPERTS])
        iota_k = sb("iota_k", [P, SORTED_TILES])
        tab_e = sb("tab_e", [P, SORTED_TILES])
        tab_ei = sb("tab_ei", [P, SORTED_TILES], INT32)
        tab_row = sb("tab_row", [P, SORTED_TILES], INT32)
        tok_i = [sb(f"tok_i{j}", [P, 1], INT32) for j in range(2)]
        w_row = [sb(f"w_row{j}", [P, 1]) for j in range(2)]
        w_tmp = sb("w_tmp", [P, 2])
        xg = [prod[:, j * ROW:(j + 1) * ROW] for j in range(2)]
        xgT = [prod[:, 1024 + j * D:1024 + (j + 1) * D] for j in range(2)]
        hg = prod[:, 2048:2048 + HALF]
        hact = prod[:, 2560:2560 + HALF]
        hgT = [prod[:, 3072 + j * HALF:3072 + (j + 1) * HALF] for j in range(2)]
        tab_first = prod_pool[:, 0:SORTED_TILES]
        bias_hi = prod_pool[:, 0:5 * D // 2].bitcast(BF16)
        yg = [prod_pool[:, j * D:(j + 1) * D] for j in range(2)]

        def bank(name):
            return ctx.enter_context(nc.psum_tensor(name, [P, 512], FP32))
        p_xT, p_q0, p_q1, p_core, p_b0, p_b1, p_b2, p_b3 = (
            bank(n) for n in ("p_xT", "p_q0", "p_q1", "p_core", "p_b0", "p_b1", "p_b2", "p_b3"))
        gate_bank, up_bank, y_bank = (p_q0, p_b0), (p_q1, p_b1), (p_b2, p_b3)

        weights_in = [sem(f"weights_in{j}") for j in range(3)]
        experts_in = sem("experts_in")
        pool_const = sem("pool_const")
        const_ready = sem("const_ready")
        xin_loaded = sem("xin_loaded")
        ln1_var = sem("ln1_var")
        ln1_std = sem("ln1_std")
        xhat_ready = sem("xhat_ready")
        scale_ready = sem("scale_ready")
        xT_psum = sem("xT_psum")
        xnT_ready = sem("xnT_ready")
        qkv_psum = sem("qkv_psum")
        qkv_taken = sem("qkv_taken")
        feat_ready = sem("feat_ready")
        pool_v_used = sem("pool_v_used")
        pool_qkv = sem("pool_qkv")
        attn_ready = sem("attn_ready")
        attnT_psum = sem("attnT_psum")
        attnT_ready = sem("attnT_ready")
        xres_loaded = sem("xres_loaded")
        a_ready = sem("a_ready")
        wo_psum = sem("wo_psum")
        ln2_var = sem("ln2_var")
        ln2_std = sem("ln2_std")
        h_ready = sem("h_ready")
        hT_psum = sem("hT_psum")
        hT_ready = sem("hT_ready")
        fc_psum = sem("fc_psum")
        gelu_ready = sem("gelu_ready")
        proj_psum = sem("proj_psum")
        x1_read = sem("x1_read")
        ln3_std = sem("ln3_std")
        rows_ready = sem("rows_ready")
        x3T_psum = sem("x3T_psum")
        x3T_ready = sem("x3T_ready")
        logits_psum = sem("logits_psum")
        gap_ready = sem("gap_ready")
        gap_exp = sem("gap_exp")
        chosen_ready = sem("chosen_ready")
        ranks_psum = sem("ranks_psum")
        slots_ready = sem("slots_ready")
        scattered = sem("scattered")
        up_psum = sem("up_psum")
        up_taken = sem("up_taken")
        shared_h = sem("shared_h")
        down_psum = sem("down_psum")
        out_ready = sem("out_ready")
        out_stored = sem("out_stored")
        dve_done = sem("dve_done")
        pool_done = sem("pool_done")
        init_stored = sem("init_stored")
        pads_at = sem("pads_at")
        pads_stored = sem("pads_stored")
        waits_passed = sem("waits_passed")
        tables_ready = sem("tables_ready")
        xg_loaded = [sem(f"xg_loaded{j}") for j in range(2)]
        xg_meta = sem("xg_meta")
        gT_psum = sem("gT_psum")
        gT_ready = sem("gT_ready")
        gu_psum = sem("gu_psum")
        g_act = sem("g_act")
        hg_ready = sem("hg_ready")
        hgT_psum = sem("hgT_psum")
        hgT_ready = sem("hgT_ready")
        y_psum = sem("y_psum")
        y_ready = sem("y_ready")
        added = sem("added")

        def wait(eng, s, value):
            if not isinstance(value, int) or value > 0:
                eng.wait_ge(s, value)

        def stand_alone(eng):
            eng.sem_inc(waits_passed, 1)

        class Chain:

            def __init__(self, eng, s):
                self.eng, self.s, self.base, self.n = eng, s, 0, 0

            def __call__(self, ins):
                self.n += 1
                ins.then_inc(self.s, 1)
                self.eng.wait_ge(self.s, self.base + self.n)

            def enter(self, done, per_round):
                self.before, self.per_round = self.base + self.n, per_round
                self.base, self.n = self.before + done * per_round, 0

            def leave(self, rounds):
                assert self.n == self.per_round, f"{self.n} steps in a round"
                self.base, self.n = self.before + rounds * self.per_round, 0

        def announce(eng, ins, s, value):
            ins.then_inc(s, 1)
            eng.wait_ge(s, value)

        FIRST, LAST = 3, BLOCKS

        def rounds(eng, body, chain=None, steps=0):
            for c in range(FIRST):
                body(c, True, c >= 1, c >= 2)
            with eng.Fori(FIRST, LAST) as c:
                if chain:
                    chain.enter(c - FIRST, steps)
                body(c, True, True, True)
                if chain:
                    chain.leave(LAST - FIRST)
            body(BLOCKS, False, True, True)
            body(BLOCKS + 1, False, False, True)

        block = ctx.enter_context(nc.Block())

        @block.sync
        def _(sp):
            sp.dma_start(xin[:], x_blk[0]).then_inc(xin_loaded, 16)
            for dst, src in ((wqkv_sb, wqkv), (ln_sb[:, 0, :], ln1w), (ln_sb[:, 1, :], ln1b),
                             (ln_sb[:, 2, :], ln2w), (ln_sb[:, 3, :], ln2b), (fcb_sb, fc_b)):
                sp.dma_start(dst[:] if dst in (wqkv_sb, fcb_sb) else dst, src).then_inc(weights_in[0], 16)
            sp.dma_start(prod[:, 0:5 * D], b_tok.to_broadcast([P, 5 * D])).then_inc(weights_in[0], 16)
            for dst, src in ((wo_sb, wo), (fc_sb, fc_w), (proj_sb, proj_w)):
                sp.dma_start(dst[:], src).then_inc(weights_in[1], 16)
            for dst, src in ((gate_sb, gate_w), (sgup_sb, sg_up), (sgdn_sb, sg_down)):
                sp.dma_start(dst[:], src).then_inc(weights_in[2], 16)
            for e in range(EXPERTS):
                sp.dma_start(exp_sb[:, e, :], experts[e]).then_inc(experts_in, 16)

            sp.wait_ge(const_ready, 1)
            sp.dma_start(rows_sorted[EXPERTS * REGION:, :].rearrange("(j p) d -> p j d", p=P),
                         pad_row[:].unsqueeze(1).to_broadcast([P, SPARE_TILES, ROW])
                         ).then_inc(init_stored, 16)
            sp.dma_start(out[TOKENS:TOKENS + P, :], pad_row[:, 0:D]).then_inc(init_stored, 16)

            def body(c, core, stage_b, tail):
                if stage_b:
                    wait(sp, x1_read, c - 1)
                    sp.dma_start(xres[:], x_blk[bass.ds(c - 1, 1)].rearrange("b p t d -> p (b t) d")
                                 ).then_inc(xres_loaded, 16)
                if core and (not isinstance(c, int) or c < BLOCKS - 1):
                    wait(sp, xT_psum, 4 * (c + 1))
                    sp.dma_start(xin[:], x_blk[bass.ds(c + 1, 1)].rearrange("b p t d -> p (b t) d")
                                 ).then_inc(xin_loaded, 16)
                if tail:
                    wait(sp, out_ready, c - 1)
                    sp.dma_start(out_blk[bass.ds(c - 2, 1)].rearrange("b p t d -> p (b t) d"), x1[:]
                                 ).then_inc(out_stored, 16)

            for c in range(FIRST):
                body(c, True, c >= 1, c >= 2)
            with sp.Fori(FIRST, LAST - 1) as c:
                body(c, True, True, True)
            body(BLOCKS - 1, True, True, True)
            body(BLOCKS, False, True, True)
            body(BLOCKS + 1, False, False, True)

            sp.wait_ge(tables_ready, 1)
            sp.wait_ge(init_stored, 32)
            sp.wait_ge(pads_stored, 16 * EXPERTS)
            sp.wait_ge(scattered, 16 * 2 * TPB * BLOCKS)

            def load(k, j):
                row = sp.value_load(tab_row[0:1, bass.ds(k, 1)], min_val=0,
                                    max_val=EXPERTS * REGION + (SPARE_TILES - 1) * P)
                wait(sp, gT_psum, k - 1)
                wait(sp, xg_meta, k - 1)
                sp.dma_start(xg[j], rows_sorted[bass.ds(row, P), :]).then_inc(xg_loaded[j], 16)
            load(0, 0)
            load(1, 1)
            with sp.Fori(1, SORTED_TILES // 2) as m:
                load(2 * m, 0)
                load(2 * m + 1, 1)
            sp.wait_ge(out_stored, 16 * BLOCKS)
            sp.wait_ge(added, 16 * SORTED_TILES)

        @block.gpsimd
        def _(pool):
            g = nc.gpsimd
            done = Chain(pool, pool_done)
            done(g.memset(ident[:], 0.0))
            g.affine_select(out=ident[:], in_=ident[:], compare_op=ALU.not_equal, fill=1.0, base=0,
                            pattern=[[-1, P]], channel_multiplier=1).then_inc(pool_const, 1)
            done(g.memset(ones_bf[:], 1.0))
            g.affine_select(out=before_bf[:], in_=ones_bf[:], compare_op=ALU.is_gt, fill=0.0, base=0,
                            pattern=[[1, P]], channel_multiplier=-1).then_inc(pool_const, 1)
            done(g.memset(v_pool[:], 1.0))
            g.iota(iota_e[:], [[1, EXPERTS]], base=0, channel_multiplier=0,
                   allow_small_or_imprecise_dtypes=True).then_inc(pool_const, 1)
            g.iota(iota_r[:], [[REGION, EXPERTS]], base=0, channel_multiplier=0,
                   allow_small_or_imprecise_dtypes=True).then_inc(pool_const, 1)
            g.iota(tok[:], [[P, TPB]], base=-BLOCK, channel_multiplier=1,
                   allow_small_or_imprecise_dtypes=True).then_inc(pool_const, 1)
            g.iota(iota_p[:], [[0, 1]], base=0, channel_multiplier=1,
                   allow_small_or_imprecise_dtypes=True).then_inc(pool_const, 1)
            g.iota(iota_k[:], [[1, SORTED_TILES]], base=0, channel_multiplier=0,
                   allow_small_or_imprecise_dtypes=True).then_inc(pool_const, 1)

            def body(c, core, stage_b, tail):
                if core:
                    wait(pool, feat_ready, 4 * c + 1)
                    done(g.tensor_tensor(
                        prod_pool[:].rearrange("p (h d e) -> p h d e", h=HEADS, d=HD),
                        fqk_pool[:, 1].unsqueeze(3).to_broadcast([P, HEADS, HD, HE]),
                        v_pool[:].unsqueeze(2).to_broadcast([P, HEADS, HD, HE]), ALU.mult))
                    w = HD * HE
                    for n in (8, 4, 2):
                        done(g.tensor_tensor(prod_pool[:, 0:n * w], prod_pool[:, 0:n * w],
                                             prod_pool[:, n * w:2 * n * w], ALU.add))
                    announce(pool, g.tensor_tensor(kv_pool[:].rearrange("p d e -> p (d e)"),
                                                   prod_pool[:, 0:w], prod_pool[:, w:2 * w],
                                                   ALU.add), pool_v_used, c + 1)
                    done(g.tensor_tensor(
                        prod_pool[:].rearrange("p (d h e) -> p d h e", d=HD, h=HEADS),
                        fqk_pool[:, 0].rearrange("p h d -> p d h").unsqueeze(3)
                        .to_broadcast([P, HD, HEADS, HE]),
                        kv_pool[:].unsqueeze(2).to_broadcast([P, HD, HEADS, HE]), ALU.mult))
                    w = HEADS * HE
                    for n in (8, 4, 2):
                        done(g.tensor_tensor(prod_pool[:, 0:n * w], prod_pool[:, 0:n * w],
                                             prod_pool[:, n * w:2 * n * w], ALU.add))
                    announce(pool, g.tensor_tensor(qkv_pool[:].rearrange("p h e -> p (h e)"),
                                                   prod_pool[:, 0:w], prod_pool[:, w:2 * w],
                                                   ALU.add), pool_qkv, c + 1)
                if stage_b:
                    wait(pool, slots_ready, c)
                    stand_alone(pool)
                    for s in range(2):
                        for t in range(TPB):
                            pool.indirect_dma_start(
                                out=rows_sorted[:, :],
                                out_offset=bass.IndirectOffsetOnAxis(
                                    ap=slot[:, s * TPB + t:s * TPB + t + 1], axis=0),
                                in_=rows[:, t, :], in_offset=None).then_inc(scattered, 16)

            rounds(pool, body, done, POOL_STEPS)

            pool.wait_ge(pads_at, 1)
            for e in range(EXPERTS):
                pool.indirect_dma_start(out=rows_sorted[:, :],
                                        out_offset=bass.IndirectOffsetOnAxis(ap=pad_at[:, e:e + 1], axis=0),
                                        in_=pad_row[:], in_offset=None).then_inc(pads_stored, 16)

            pool.wait_ge(out_stored, 16 * BLOCKS)
            pool.wait_ge(init_stored, 32)

            def add(k, j):
                pool.wait_ge(y_ready, k + 1)
                wait(pool, added, 16 * k)
                stand_alone(pool)
                pool.indirect_dma_start(out=out[:, :],
                                        out_offset=bass.IndirectOffsetOnAxis(ap=tok_i[j][:], axis=0),
                                        in_=yg[j], in_offset=None, compute_op=ALU.add).then_inc(added, 16)
            add(0, 0)
            add(1, 1)
            with pool.Fori(1, SORTED_TILES // 2) as m:
                add(2 * m, 0)
                add(2 * m + 1, 1)

        @block.scalar
        def _(act):
            a = nc.scalar

            def take_x(c, u):
                n = 4 * c + u
                wait(act, xT_psum, n + 1)
                wait(act, qkv_psum, n - 1)
                for k in range(KC):
                    ins = a.activation(xnT[u % 2][:, k, :], p_xT[:, k * P:(k + 1) * P], ACT.Identity,
                                       bias=ln_sb[:, 1, k:k + 1], scale=ln_sb[:, 0, k:k + 1])
                ins.then_inc(xnT_ready, 1)

            def take_qkv(c, u):
                n = 4 * c + u
                wait(act, qkv_psum, n + 1)
                wait(act, feat_ready, n)
                a.activation(eqk[:], p_q0[:], ACT.Exp)
                a.activation(rqk[:], p_q0[:], ACT.Relu)
                v = p_q1[:, 0:D].rearrange("p (h e) -> p h e", h=HEADS)
                if u == 0:
                    wait(act, pool_v_used, c)
                    ins = a.activation(v_pool[:, :, 0:HD], v, ACT.Copy)
                else:
                    ins = a.activation(v_dve[u % 2][:].rearrange("p e h -> p h e"), v, ACT.Copy)
                ins.then_inc(qkv_taken, 1)

            def body(c, core, stage_b, tail):
                if stage_b:
                    wait(act, xres_loaded, 16 * c)
                    wait(act, scale_ready, c)
                    wait(act, hT_psum, c - 1)
                    for t in range(TPB):
                        ins = a.activation(xmid[:, t, :], xres[:, t, :], ACT.Identity,
                                           bias=a_scale[:, 1, t:t + 1], scale=a_scale[:, 0, t:t + 1])
                    ins.then_inc(a_ready, 1)
                if core:
                    take_qkv(c, 1)
                if stage_b:
                    wait(act, attnT_psum, c)
                    a.activation(bT[:, 0, :], p_b0[:], ACT.Copy)
                    a.activation(bT[:, 1, :], p_b1[:], ACT.Copy).then_inc(attnT_ready, 1)
                if core:
                    take_x(c, 2)
                    take_x(c, 3)
                    take_qkv(c, 2)
                if stage_b:
                    wait(act, ln2_var, c)
                    a.activation(sq_b[:], sq_b[:], ACT.Sqrt).then_inc(ln2_std, 1)
                if core and (not isinstance(c, int) or c < BLOCKS - 1):
                    wait(act, ln1_var, c + 2)
                    a.activation(sq_a[:], sq_a[:], ACT.Sqrt).then_inc(ln1_std, 1)
                if stage_b:
                    wait(act, hT_psum, c)
                    for k, bnk in enumerate((p_b2, p_b3)):
                        ins = a.activation(bT[:, k, :], bnk[:], ACT.Identity,
                                           bias=ln_sb[:, 3, k:k + 1], scale=ln_sb[:, 2, k:k + 1])
                    ins.then_inc(hT_ready, 1)
                    for f in range(FCH):
                        wait(act, fc_psum, FCH * (c - 1) + f + 1)
                        a.activation(hid[:, f, :], (p_b2, p_b3)[f % 2][:], ACT.Gelu,
                                     bias=fcb_sb[:, f:f + 1]).then_inc(gelu_ready, 1)
                if core:
                    take_qkv(c, 3)
                if core and (not isinstance(c, int) or c < BLOCKS - 1):
                    take_x(c + 1, 0)
                    take_x(c + 1, 1)
                    take_qkv(c + 1, 0)
                if stage_b:
                    wait(act, x1_read, c)
                    a.activation(sq_b[:], sq_b[:], ACT.Sqrt).then_inc(ln3_std, 1)
                    wait(act, x3T_psum, c)
                    a.activation(bT[:, 0, :], p_b2[:], ACT.Copy)
                    a.activation(bT[:, 1, :], p_b3[:], ACT.Copy).then_inc(x3T_ready, 1)
                    wait(act, gap_ready, c)
                    a.activation(gap_e[:], gap[:], ACT.Exp).then_inc(gap_exp, 1)
                    for f in range(HCH):
                        wait(act, up_psum, HCH * (c - 1) + f + 1)
                        a.activation(sg_g[:, f, :], p_b2[:], ACT.Silu)
                        a.activation(sg_u[:, f, :], p_b3[:], ACT.Copy).then_inc(up_taken, 1)

            act.wait_ge(weights_in[0], 16 * 7)
            act.wait_ge(pool_const, 3)
            wait(act, ln1_var, 1)
            a.activation(sq_a[:], sq_a[:], ACT.Sqrt).then_inc(ln1_std, 1)
            take_x(0, 0)
            take_x(0, 1)
            take_qkv(0, 0)
            for c in range(FIRST):
                body(c, True, c >= 1, c >= 2)
            with act.Fori(FIRST, LAST - 1) as c:
                body(c, True, True, True)
            body(BLOCKS - 1, True, True, True)
            body(BLOCKS, False, True, True)

            def take_gT(k, j):
                act.wait_ge(gT_psum, k + 1)
                wait(act, gu_psum, k - 1)
                a.activation(xgT[j], p_xT[:, 0:D], ACT.Copy).then_inc(gT_ready, 1)

            def silu(k, j):
                act.wait_ge(gu_psum, k + 1)
                wait(act, hg_ready, k)
                a.activation(hact, gate_bank[j][:, 0:HALF], ACT.Silu).then_inc(g_act, 1)

            def weigh(k, j):
                act.wait_ge(y_psum, k + 1)
                wait(act, xg_meta, k + 1)
                wait(act, added, 16 * (k - 1))
                a.activation(yg[j], y_bank[j][:, 0:D], ACT.Copy, scale=w_row[j][:, 0:1]).then_inc(y_ready, 1)

            act.wait_ge(tables_ready, 1)
            take_gT(0, 0)
            silu(0, 0)
            take_gT(1, 1)

            def pair(k, j):
                silu(k, j)
                weigh(k - 1, 1 - j)
                take_gT(k + 1, 1 - j)
            pair(1, 1)
            pair(2, 0)
            with act.Fori(1, (SORTED_TILES - 2) // 2) as m:
                pair(2 * m + 1, 1)
                pair(2 * m + 2, 0)
            silu(SORTED_TILES - 1, 1)
            weigh(SORTED_TILES - 2, 0)
            weigh(SORTED_TILES - 1, 1)

        @block.vector
        def _(dve):
            v = nc.vector
            done = Chain(dve, dve_done)

            def stats(src, mv):
                for t in range(TPB):
                    v.bn_stats(st6[:, t, :], src(t)).then_inc(dve_done, 1)
                    done.n += 1
                dve.wait_ge(dve_done, done.base + done.n)
                stand_alone(dve)
                for t in range(TPB):
                    ins = v.bn_aggr(mv[:, t, :], st6[:, t, :])
                    if t < TPB - 1:
                        ins.then_inc(dve_done, 1)
                        done.n += 1
                done(ins)

            def ln1_stats(b):
                wait(dve, xin_loaded, 16 * (b + 1))
                stats(lambda t: xin[:, t, :], mv_a)
                done(v.tensor_scalar(sq_a[:, 0, :], mv_a[:, :, 1], 1.0, EPS, ALU.mult, ALU.add))
                announce(dve, v.tensor_scalar(sq_a[:, 1, :], mv_a[:, :, 1], 1.0 + EPS, EPS * EPS,
                                              ALU.mult, ALU.add), ln1_var, b + 1)

            def ln1_norm(b):
                wait(dve, ln1_std, b + 1)
                done(v.reciprocal(rs_a[:], sq_a[:]))
                for t in range(TPB):
                    ins = v.tensor_scalar(xin[:, t, :], xin[:, t, :], mv_a[:, t, 0:1],
                                          rs_a[:, 1, t:t + 1], ALU.subtract, ALU.mult)
                    if t < TPB - 1:
                        done(ins)
                announce(dve, ins, xhat_ready, b + 1)

            def keep_scales(c):
                wait(dve, a_ready, c)
                done(v.tensor_copy(a_scale[:, 0, :], rs_a[:, 0, :]))
                announce(dve, v.scalar_tensor_tensor(a_scale[:, 1, :], mv_a[:, :, 0], -1.0, rs_a[:, 0, :],
                                                     ALU.mult, ALU.mult), scale_ready, c + 1)

            def features(c, u):
                n = 4 * c + u
                wait(dve, qkv_taken, n + 1)
                if u == 0:
                    ins = v.scalar_tensor_tensor(fqk_pool[:].rearrange("p a h d -> p (a h d)"), eqk[:], 1.0,
                                                 rqk[:], ALU.min, ALU.add)
                else:
                    done(v.scalar_tensor_tensor(fq[:].rearrange("p h d -> p (h d)"), eqk[:, 0:D], 1.0,
                                                rqk[:, 0:D], ALU.min, ALU.add))
                    ins = v.scalar_tensor_tensor(
                        fkT, eqk[:, D:2 * D].rearrange("p (h d) -> p d h", h=HEADS), 1.0,
                        rqk[:, D:2 * D].rearrange("p (h d) -> p d h", h=HEADS), ALU.min, ALU.add)
                announce(dve, ins, feat_ready, n + 1)

            fkT = p_core[:, 0:D].rearrange("p (d h) -> p d h", d=HD)
            kv_first = 512 - HE * HD
            kvT = p_core[:, kv_first:512].rearrange("p (e d) -> p e d", e=HE)

            def kv_products(u):
                done(v.tensor_reduce(kvT[:, HD, :], fkT, AX.X, ALU.add))
                done(v.tensor_tensor(
                    prod[:, 0:HD * HD * HEADS].rearrange("p (e d h) -> p e d h", e=HD, d=HD),
                    fkT.unsqueeze(1).to_broadcast([P, HD, HD, HEADS]),
                    v_dve[u % 2][:].unsqueeze(2).to_broadcast([P, HD, HD, HEADS]), ALU.mult))

            def kv_sums():
                done(v.tensor_reduce(
                    p_core[:, kv_first:kv_first + HD * HD],
                    prod[:, 0:HD * HD * HEADS].rearrange("p (a h) -> p a h", h=HEADS), AX.X, ALU.add))

            def q_products():
                done(v.tensor_tensor(
                    prod[:].rearrange("p (h e d) -> p h e d", h=HEADS, e=HE),
                    fq[:].unsqueeze(2).to_broadcast([P, HEADS, HE, HD]),
                    kvT.unsqueeze(1).to_broadcast([P, HEADS, HE, HD]), ALU.mult))

            def q_sums():
                done(v.tensor_reduce(qkv[:].rearrange("p h e -> p (h e)"),
                                     prod[:].rearrange("p (a d) -> p a d", d=HD), AX.X, ALU.add))

            def divide(c, t, src):
                done(v.tensor_scalar(den[:], src[:, :, HD], 1e-6, None, ALU.add))
                done(v.reciprocal(den[:], den[:]))
                wait(dve, attnT_psum, c)
                return v.tensor_tensor(attn[:, t, :].rearrange("p (h e) -> p h e", h=HEADS),
                                       src[:, :, 0:HD],
                                       den[:].unsqueeze(2).to_broadcast([P, HEADS, HD]), ALU.mult)

            def residual_1(c):
                wait(dve, a_ready, c)
                wait(dve, wo_psum, c)
                flat = xmid[:].rearrange("p t d -> p (t d)")
                for k, bnk in enumerate((p_b2, p_b3)):
                    done(v.tensor_tensor(flat[:, 512 * k:512 * k + 512], flat[:, 512 * k:512 * k + 512],
                                         bnk[:], ALU.add))
                wait(dve, xres_loaded, 16 * c)
                done(v.tensor_tensor(xres[:], xres[:], xmid[:], ALU.add))
                stats(lambda t: xmid[:, t, :], mv_b)
                announce(dve, v.tensor_scalar(sq_b[:], mv_b[:, :, 1], 1.0, EPS, ALU.mult, ALU.add),
                         ln2_var, c)

            def norm_2(c):
                wait(dve, ln2_std, c)
                done(v.reciprocal(rs_b[:], sq_b[:]))
                for t in range(TPB):
                    ins = v.tensor_scalar(xmid[:, t, :], xmid[:, t, :], mv_b[:, t, 0:1], rs_b[:, t:t + 1],
                                          ALU.subtract, ALU.mult)
                    if t < TPB - 1:
                        done(ins)
                announce(dve, ins, h_ready, c)

            def residual_2(c):
                wait(dve, proj_psum, c)
                wait(dve, out_stored, 16 * (c - 1))
                flat, res = (z[:].rearrange("p t d -> p (t d)") for z in (x1, xres))
                for k, bnk in enumerate((p_b0, p_b1)):
                    done(v.tensor_tensor(flat[:, 512 * k:512 * k + 512], res[:, 512 * k:512 * k + 512],
                                         bnk[:], ALU.add))
                stats(lambda t: x1[:, t, :], mv_b)
                announce(dve, v.tensor_scalar(sq_b[:], mv_b[:, :, 1], 1.0, EPS, ALU.mult, ALU.add),
                         x1_read, c)

            def norm_3(c):
                wait(dve, ln3_std, c)
                done(v.reciprocal(rs_b[:], sq_b[:]))
                wait(dve, scattered, 16 * 2 * TPB * (c - 1))
                for t in range(TPB):
                    ins = v.tensor_scalar(rows[:, t, 0:D], x1[:, t, :], mv_b[:, t, 0:1], rs_b[:, t:t + 1],
                                          ALU.subtract, ALU.mult)
                    if t < TPB - 1:
                        done(ins)
                announce(dve, ins, rows_ready, c)

            def choose(c):
                wait(dve, logits_psum, c)
                done(v.tensor_copy(logit[:].rearrange("p t e -> p (t e)"), p_b0[:, 0:TPB * EXPERTS]))
                for t in range(TPB):
                    stand_alone(dve)
                    done(v.max(top_v[:, t, :], logit[:, t, :]))
                announce(dve, v.tensor_tensor(gap[:], top_v[:, :, 1], top_v[:, :, 0], ALU.subtract),
                         gap_ready, c)
                for t in range(TPB):
                    stand_alone(dve)
                    done(v.max_index(top_i[:, t, :], top_v[:, t, :], logit[:, t, :]))
                done(v.tensor_copy(first2[:], top_i[:, :, 0:2].rearrange("p t s -> p s t")))
                for s in range(2):
                    done(v.tensor_tensor(
                        onehot[:, s], iota_e[:].unsqueeze(1).to_broadcast([P, TPB, EXPERTS]),
                        first2[:, s, :].unsqueeze(2).to_broadcast([P, TPB, EXPERTS]), ALU.is_equal))
                announce(dve, v.tensor_tensor(chosen[:], onehot[:, 0], onehot[:, 1], ALU.add),
                         chosen_ready, c)

            def place(c):
                n = TPB * EXPERTS
                wait(dve, ranks_psum, c)
                done(v.tensor_tensor(rank[:], p_b1[:, 0:n].rearrange("p (t e) -> p t e", t=TPB),
                                     free_row[:].unsqueeze(1).to_broadcast([P, TPB, EXPERTS]), ALU.add))
                done(v.tensor_tensor(free_row[:], free_row[:], p_b1[:, n:n + EXPERTS], ALU.add))
                done(v.tensor_tensor(
                    slot_w[:].rearrange("p s t e -> p s (t e)"),
                    onehot[:].rearrange("p s t e -> p s (t e)"),
                    rank[:].rearrange("p t e -> p (t e)").unsqueeze(1).to_broadcast([P, 2, n]), ALU.mult))
                with nc.allow_low_precision(reason="row numbers are whole and below 2^24"):
                    done(v.tensor_reduce(slot[:], slot_w[:].rearrange("p s t e -> p (s t) e"), AX.X, ALU.add))
                done(v.tensor_scalar(tok[:], tok[:], float(BLOCK), None, ALU.add))
                done(v.tensor_copy(rows[:, :, C_TOK], tok[:]))
                done(v.tensor_copy(rows[:, :, C_E0], first2[:, 0, :]))
                wait(dve, gap_exp, c)
                done(v.tensor_scalar(gap[:], gap_e[:], 1.0, None, ALU.add))
                done(v.reciprocal(gap[:], gap[:]))
                done(v.tensor_copy(rows[:, :, C_W0], gap[:]))
                announce(dve, v.tensor_tensor(rows[:, :, C_W1], gap_e[:], gap[:], ALU.mult), slots_ready, c)

            def shared_hidden(c):
                wait(dve, up_taken, HCH * (c - 1))
                announce(dve, v.tensor_tensor(sg_g, sg_g, sg_u, ALU.mult), shared_h, c - 1)

            def finish(c):
                wait(dve, down_psum, c - 1)
                flat = x1[:].rearrange("p t d -> p (t d)")
                done(v.tensor_tensor(flat[:, 0:512], flat[:, 0:512], p_b0[:], ALU.add))
                announce(dve, v.tensor_tensor(flat[:, 512:1024], flat[:, 512:1024], p_b1[:], ALU.add),
                         out_ready, c - 1)

            def body(c, core, stage_b, tail):
                last = isinstance(c, int) and c >= BLOCKS - 1
                if core:
                    features(c, 0)
                    features(c, 1)
                    kv_products(1)
                    kv_sums()
                if stage_b:
                    residual_1(c)
                if tail:
                    shared_hidden(c)
                if core:
                    q_products()
                    keep_scales(c)
                    if not last:
                        ln1_stats(c + 1)
                if stage_b:
                    norm_2(c)
                if core:
                    if not last:
                        ln1_norm(c + 1)
                    q_sums()
                    done(divide(c, 0, qkv))
                    features(c, 2)
                    kv_products(2)
                if tail:
                    finish(c)
                if core:
                    kv_sums()
                    q_products()
                    q_sums()
                    done(divide(c, 1, qkv))
                    features(c, 3)
                    kv_products(3)
                if stage_b:
                    residual_2(c)
                if core:
                    kv_sums()
                if stage_b:
                    norm_3(c)
                if core:
                    q_products()
                if stage_b:
                    choose(c)
                if core:
                    q_sums()
                    done(divide(c, 2, qkv))
                    wait(dve, pool_qkv, c + 1)
                    announce(dve, divide(c, POOL_TILE, qkv_pool), attn_ready, c + 1)
                if stage_b:
                    place(c)

            dve.wait_ge(weights_in[0], 16 * 7)
            dve.wait_ge(pool_const, 7)
            left = prod[:, 0:5 * D]
            part = prod[:, 5 * D:10 * D]
            done(v.memset(bias_bf[:], 0.0))
            for row in (0, 32, 64):
                done(v.tensor_copy(bias_bf[row:row + 1, :], left[row:row + 1, :]))
                if row < 64:
                    done(v.tensor_copy(bias_hi, left))
                    done(v.tensor_copy(part, bias_hi))
                    done(v.tensor_tensor(left, left, part, ALU.subtract))
            done(v.tensor_copy(free_row[:], iota_r[:]))
            done(v.memset(pad_row[:], 0.0))
            done(v.tensor_scalar(pad_row[:, C_TOK:C_TOK + 1], iota_p[:], float(TOKENS), None, ALU.add))
            announce(dve, v.memset(den[:], 0.0), const_ready, 1)
            ln1_stats(0)
            ln1_norm(0)

            for c in range(FIRST):
                body(c, True, c >= 1, c >= 2)
            with dve.Fori(FIRST, LAST - 1) as c:
                done.enter(c - FIRST, DVE_STEPS)
                body(c, True, True, True)
                done.leave(LAST - 1 - FIRST)
            body(BLOCKS - 1, True, True, True)
            body(BLOCKS, False, True, True)
            body(BLOCKS + 1, False, False, True)

            announce(dve, v.tensor_scalar(pad_at[:], free_row[:], iota_p[:, 0:1], None, ALU.add), pads_at, 1)
            done(v.tensor_tensor(tiles_f[:], free_row[:], iota_r[:], ALU.subtract))
            done(v.tensor_scalar(cnt_i[:], tiles_f[:], float(P - 1), None, ALU.add))
            done(v.tensor_scalar(cnt_i[:], cnt_i[:], P.bit_length() - 1, None, ALU.arith_shift_right))
            done(v.tensor_copy(tiles_f[:], cnt_i[:]))
            done(v.tensor_copy(tiles_to[:], tiles_f[:]))
            for e in range(1, EXPERTS):
                done(v.tensor_tensor(tiles_to[:, e:e + 1], tiles_to[:, e:e + 1], tiles_to[:, e - 1:e], ALU.add))
            over = prod[:, 0:SORTED_TILES * EXPERTS].rearrange("p (k e) -> p k e", e=EXPERTS)
            wide = [P, SORTED_TILES, EXPERTS]
            done(v.tensor_tensor(over, iota_k[:].unsqueeze(2).to_broadcast(wide),
                                 tiles_to[:].unsqueeze(1).to_broadcast(wide), ALU.is_ge))
            done(v.tensor_reduce(tab_e[:], over, AX.X, ALU.add))
            done(v.tensor_scalar(tab_ei[:], tab_e[:], float(EXPERTS - 1), None, ALU.min))
            done(v.tensor_tensor(over, over, tiles_f[:].unsqueeze(1).to_broadcast(wide), ALU.mult))
            done(v.tensor_reduce(tab_first, over, AX.X, ALU.add))
            done(v.tensor_tensor(tab_first, iota_k[:], tab_first, ALU.subtract))
            done(v.tensor_scalar(tab_first, tab_first, float(P), None, ALU.mult))
            announce(dve, v.scalar_tensor_tensor(tab_row[:], tab_e[:], float(REGION), tab_first,
                                                 ALU.mult, ALU.add), tables_ready, 1)

            def meta(k, j):
                dve.wait_ge(xg_loaded[j], 16 * (k // 2 + 1) if isinstance(k, int) else 8 * (k - j) + 16)
                wait(dve, added, 16 * (k - 1))
                row = xg[j]
                done(v.tensor_copy(tok_i[j][:], row[:, C_TOK:C_TOK + 1]))
                done(v.tensor_tensor(w_tmp[:, 0:1], row[:, C_E0:C_E0 + 1], tab_e[:, bass.ds(k, 1)], ALU.is_equal))
                done(v.scalar_tensor_tensor(w_tmp[:, 1:2], w_tmp[:, 0:1], 0.0, row[:, C_W1:C_W1 + 1],
                                            ALU.is_equal, ALU.mult))
                announce(dve, v.scalar_tensor_tensor(w_row[j][:], row[:, C_W0:C_W0 + 1], w_tmp[:, 0:1],
                                                     w_tmp[:, 1:2], ALU.mult, ALU.add), xg_meta, k + 1)

            def gated(k, j):
                dve.wait_ge(g_act, k + 1)
                wait(dve, hgT_psum, k)
                announce(dve, v.tensor_tensor(hg, hact, up_bank[j][:, 0:HALF], ALU.mult), hg_ready, k + 1)

            def take_hT(k, j):
                dve.wait_ge(hgT_psum, k + 1)
                wait(dve, y_psum, k - 1)
                announce(dve, v.tensor_copy(hgT[j], p_core[:, 0:HALF]), hgT_ready, k + 1)

            def tile(k, j):
                meta(k, j)
                gated(k, j)
                take_hT(k, j)
            tile(0, 0)
            tile(1, 1)
            with dve.Fori(1, SORTED_TILES // 2) as m:
                done.enter(m - 1, 6)
                tile(2 * m, 0)
                tile(2 * m + 1, 1)
                done.leave(SORTED_TILES // 2 - 1)

        @block.tensor
        def _(pe):
            t_ = nc.tensor

            def project_x(c, u, part):
                n = 4 * c + u
                if part == "T":
                    wait(pe, xhat_ready, c + 1)
                    wait(pe, xnT_ready, n)
                    for k in range(KC):
                        ins = t_.transpose(p_xT[:, k * P:(k + 1) * P],
                                           xin[:, ORDER[u], k * P:(k + 1) * P], ident[:])
                    ins.then_inc(xT_psum, 1)
                else:
                    wait(pe, xnT_ready, n + 1)
                    wait(pe, qkv_taken, n)
                    for bnk, lo, hi in ((p_q0, 0, 512), (p_q1, 512, 768)):
                        for k in range(KC):
                            t_.matmul(bnk[:, 0:hi - lo], xnT[u % 2][:, k, :], wqkv_sb[:, k, lo:hi],
                                      start=k == 0, stop=False)
                        ins = t_.matmul(bnk[:, 0:hi - lo], ones_bf[:], bias_bf[:, lo:hi],
                                        start=False, stop=True)
                    ins.then_inc(qkv_psum, 1)

            def transpose_block(src, banks, ready):
                for k, bnk in enumerate(banks):
                    for t in range(TPB):
                        ins = t_.transpose(bnk[:, t * P:(t + 1) * P], src[:, t, k * P:(k + 1) * P], ident[:])
                ins.then_inc(ready, 1)

            def to_tokens(src, chunks, w, banks, bias_at, ready):
                for t in range(TPB):
                    o = banks[t // 2][:, (t % 2) * D:(t % 2 + 1) * D]
                    for k in range(chunks):
                        ins = t_.matmul(o, src[:, k, t * P:(t + 1) * P], w[:, k, :], start=k == 0,
                                        stop=bias_at is None and k == chunks - 1)
                    if bias_at is not None:
                        ins = t_.matmul(o, ones_bf[:], bias_bf[:, bias_at:bias_at + D], start=False, stop=True)
                ins.then_inc(ready, 1)

            def body(c, core, stage_b, tail):
                last = isinstance(c, int) and c >= BLOCKS - 1
                if stage_b:
                    wait(pe, attn_ready, c)
                    wait(pe, slots_ready, c - 1)
                    transpose_block(attn, (p_b0, p_b1), attnT_psum)
                if core:
                    project_x(c, 1, "P")
                if stage_b:
                    wait(pe, attnT_ready, c)
                    wait(pe, up_taken, HCH * (c - 1))
                    to_tokens(bT, KC, wo_sb, (p_b2, p_b3), 3 * D, wo_psum)
                if core:
                    project_x(c, 2, "T")
                    project_x(c, 3, "T")
                    project_x(c, 2, "P")
                if tail:
                    wait(pe, shared_h, c - 1)
                    if stage_b:
                        wait(pe, attnT_ready, c)
                    else:
                        wait(pe, slots_ready, c - 1)
                    to_tokens(sg_g, HCH, sgdn_sb, (p_b0, p_b1), None, down_psum)
                if stage_b:
                    wait(pe, h_ready, c)
                    transpose_block(xmid, (p_b2, p_b3), hT_psum)
                    wait(pe, hT_ready, c)
                    for f in range(FCH):
                        if f >= 2:
                            wait(pe, gelu_ready, FCH * (c - 1) + f - 1)
                        bnk = (p_b2, p_b3)[f % 2]
                        for k in range(KC):
                            ins = t_.matmul(bnk[:], fc_sb[:, k, f * P:(f + 1) * P], bT[:, k, :],
                                            start=k == 0, stop=k == KC - 1)
                        ins.then_inc(fc_psum, 1)
                if core:
                    project_x(c, 3, "P")
                if stage_b:
                    wait(pe, gelu_ready, FCH * c)
                    wait(pe, out_ready, c - 1)
                    to_tokens(hid, FCH, proj_sb, (p_b0, p_b1), 4 * D, proj_psum)
                if core and not last:
                    project_x(c + 1, 0, "T")
                    project_x(c + 1, 1, "T")
                    project_x(c + 1, 0, "P")
                if stage_b:
                    wait(pe, rows_ready, c)
                    transpose_block(rows, (p_b2, p_b3), x3T_psum)
                    wait(pe, x3T_ready, c)
                    for t in range(TPB):
                        for k in range(KC):
                            ins = t_.matmul(p_b0[:, t * EXPERTS:(t + 1) * EXPERTS],
                                            bT[:, k, t * P:(t + 1) * P], gate_sb[:, k, :],
                                            start=k == 0, stop=k == KC - 1)
                    ins.then_inc(logits_psum, 1)
                    for f in range(HCH):
                        if f:
                            wait(pe, up_taken, HCH * (c - 1) + f)
                        for bnk, lo in ((p_b2, f * P), (p_b3, HALF + f * P)):
                            for k in range(KC):
                                ins = t_.matmul(bnk[:], sgup_sb[:, k, lo:lo + P], bT[:, k, :],
                                                start=k == 0, stop=k == KC - 1)
                        ins.then_inc(up_psum, 1)
                        if f == 0:
                            wait(pe, chosen_ready, c)
                            for t in range(TPB):
                                o = p_b1[:, t * EXPERTS:(t + 1) * EXPERTS]
                                for s in range(t):
                                    t_.matmul(o, ones_bf[:], chosen[:, s, :], start=s == 0, stop=False)
                                t_.matmul(o, before_bf[:], chosen[:, t, :], start=t == 0, stop=True)
                            o = p_b1[:, TPB * EXPERTS:(TPB + 1) * EXPERTS]
                            for t in range(TPB):
                                ins = t_.matmul(o, ones_bf[:], chosen[:, t, :], start=t == 0, stop=t == TPB - 1)
                            ins.then_inc(ranks_psum, 1)

            pe.wait_ge(pool_const, 7)
            pe.wait_ge(const_ready, 1)
            pe.wait_ge(weights_in[0], 16 * 7)
            pe.wait_ge(weights_in[1], 16 * 3)
            pe.wait_ge(weights_in[2], 16 * 3)
            project_x(0, 0, "T")
            project_x(0, 1, "T")
            project_x(0, 0, "P")
            for c in range(FIRST):
                body(c, True, c >= 1, c >= 2)
            with pe.Fori(FIRST, LAST - 1) as c:
                body(c, True, True, True)
            body(BLOCKS - 1, True, True, True)
            body(BLOCKS, False, True, True)
            body(BLOCKS + 1, False, False, True)

            def expert(k):
                return pe.value_load(tab_ei[0:1, bass.ds(k, 1)], min_val=0, max_val=EXPERTS - 1)

            def exp_w(e, lo, hi):
                return exp_sb[:, bass.ds(e, 1), lo:hi].rearrange("p a n -> p (a n)")

            def gT(k, j):
                pe.wait_ge(xg_loaded[j], 16 * (k // 2 + 1) if isinstance(k, int) else 8 * (k - j) + 16)
                wait(pe, gT_ready, k)
                for c in range(KC):
                    ins = t_.transpose(p_xT[:, c * P:(c + 1) * P], xg[j][:, c * P:(c + 1) * P], ident[:])
                ins.then_inc(gT_psum, 1)

            def gate_up(k, j):
                e = expert(k)
                pe.wait_ge(gT_ready, k + 1)
                wait(pe, hg_ready, k - 1)
                for bnk, lo in ((gate_bank[j], 0), (up_bank[j], HALF)):
                    for c in range(KC):
                        at = c * 2 * HALF + lo
                        ins = t_.matmul(bnk[:, 0:HALF], xgT[j][:, c * P:(c + 1) * P],
                                        exp_w(e, at, at + HALF), start=c == 0, stop=c == KC - 1)
                ins.then_inc(gu_psum, 1)

            def hT(k, j):
                pe.wait_ge(hg_ready, k + 1)
                wait(pe, hgT_ready, k)
                for c in range(HCH):
                    ins = t_.transpose(p_core[:, c * P:(c + 1) * P], hg[:, c * P:(c + 1) * P], ident[:])
                ins.then_inc(hgT_psum, 1)

            def down(k, j):
                e = expert(k)
                pe.wait_ge(hgT_ready, k + 1)
                wait(pe, y_ready, k - 1)
                for c in range(HCH):
                    at = KC * 2 * HALF + c * D
                    ins = t_.matmul(y_bank[j][:, 0:D], hgT[j][:, c * P:(c + 1) * P], exp_w(e, at, at + D),
                                    start=c == 0, stop=c == HCH - 1)
                ins.then_inc(y_psum, 1)

            pe.wait_ge(tables_ready, 1)
            pe.wait_ge(experts_in, 16 * EXPERTS)
            gT(0, 0)
            gate_up(0, 0)
            gT(1, 1)
            hT(0, 0)

            def tile(k, j):
                gate_up(k, j)
                down(k - 1, 1 - j)
                gT(k + 1, 1 - j)
                hT(k, j)
            tile(1, 1)
            tile(2, 0)
            with pe.Fori(1, (SORTED_TILES - 2) // 2) as m:
                tile(2 * m + 1, 1)
                tile(2 * m + 2, 0)
            k = SORTED_TILES - 1
            gate_up(k, 1)
            down(k - 1, 0)
            hT(k, 1)
            down(k, 1)


def kernel(**inputs):
    import numpy as np
    import concourse.bacc as bacc
    from concourse.bass_utils import run_bass_kernel_spmd

    def get(name):
        return np.asarray(inputs["L0_" + name])

    def rows_of(w):
        return w.reshape(-1, P, w.shape[-1]).transpose(1, 0, 2)

    w_up, w_down = get("ffn_w_up"), get("ffn_w_down")
    experts = np.concatenate([
        w_up.transpose(0, 2, 1).reshape(EXPERTS, KC, P, 2 * HALF).transpose(0, 2, 1, 3).reshape(EXPERTS, P, -1),
        w_down.transpose(0, 2, 1).reshape(EXPERTS, HCH, P, D).transpose(0, 2, 1, 3).reshape(EXPERTS, P, -1),
    ], axis=2)
    arrays = {
        "x": get("attn_q_x").reshape(TOKENS, D),
        "wqkv": rows_of(np.concatenate([get("attn_wq"), get("attn_wk"), get("attn_wv")], axis=1)),
        "b_tok": np.concatenate([get(f"attn_{n}") for n in ("bq", "bk", "bv", "bo", "proj_b")])[None],
        "ln1w": get("attn_ln1_w").reshape(KC, P).T,
        "ln1b": get("attn_ln1_b").reshape(KC, P).T,
        "ln2w": get("attn_ln2_w").reshape(KC, P).T,
        "ln2b": get("attn_ln2_b").reshape(KC, P).T,
        "wo": rows_of(get("attn_wo")),
        "fc_w": rows_of(get("attn_fc_w")),
        "fc_b": get("attn_fc_b").reshape(FCH, P).T,
        "proj_w": rows_of(get("attn_proj_w")),
        "gate_w": rows_of(get("ffn_gate_w").T),
        "sg_up": rows_of(np.concatenate([get("ffn_sg_gate"), get("ffn_sg_up")], axis=0).T),
        "sg_down": rows_of(get("ffn_sg_down").T),
        "experts": experts,
    }
    nc = bacc.Bacc("TRN2", target_bir_lowering=False, num_devices=1)
    feeds, args = {}, []
    for name, a in arrays.items():
        feeds[f"in_{name}"] = np.ascontiguousarray(a)
        args.append(nc.dram_tensor(f"in_{name}", list(a.shape), mybir.dt.from_np(a.dtype),
                                   kind="ExternalInput").ap())
    args.append(nc.dram_tensor("out_rows", [TOKENS + P, D], FP32, kind="ExternalOutput").ap())
    build(nc, *args)
    result = run_bass_kernel_spmd(nc, [feeds], core_ids=[0]).results[0]
    return result["out_rows"][0:TOKENS].reshape(16, 512, D)
```

```python
from contextlib import ExitStack

import concourse.bass as bass
from concourse import mybir

FP32 = mybir.dt.float32
BF16 = mybir.dt.bfloat16
INT32 = mybir.dt.int32
UINT32 = mybir.dt.uint32
ALU = mybir.AluOpType
ACT = mybir.ActivationFunctionType
AX = mybir.AxisListType

P = 128
TOKENS = 16 * 512
D = 256
KC = D // P
HEADS = 16
HD = D // HEADS
MLP = 4 * D
FCH = MLP // P
EXPERTS = 8
HALF = 384
HCH = HALF // P
TPB = 4
BLOCK = TPB * P
BLOCKS = TOKENS // BLOCK
EPS = 1e-5

REGION = TOKENS + P
SORTED_TILES = 2 * TOKENS // P + EXPERTS
SPARE_TILES = EXPERTS
ROW = D + 4
C_TOK, C_W0, C_W1, C_E0 = D, D + 1, D + 2, D + 3
EXW = KC * 2 * HALF + HCH * D

POOL_TILE = 3
POOL_HEADS = 4
DVE_HEADS = HEADS - POOL_HEADS
ORDER = (POOL_TILE, 0, 1, 2)
POOL_STEPS, DVE_STEPS = 23, 82
HE = HD + 1


def build(nc, x, wqkv, b_tok, ln1w, ln1b, ln2w, ln2b, wo, fc_w, fc_b, proj_w, gate_w, sg_up, sg_down,
          experts, out):
    ctx = ExitStack()
    with ctx:
        def sb(name, shape, dt=FP32):
            return ctx.enter_context(nc.sbuf_tensor(name, shape, dt))

        def sem(name):
            return ctx.enter_context(nc.semaphore(name))

        x_blk = x.rearrange("(b t p) d -> b p t d", t=TPB, p=P)
        out_blk = out[0:TOKENS, :].rearrange("(b t p) d -> b p t d", t=TPB, p=P)
        rows_sorted = nc.dram_tensor("rows_sorted", [EXPERTS * REGION + SPARE_TILES * P, ROW], FP32,
                                     kind="Internal").ap()

        wqkv_sb = sb("wqkv_sb", [P, KC, 3 * D])
        wo_sb = sb("wo_sb", [P, KC, D])
        fc_sb = sb("fc_sb", [P, KC, MLP])
        proj_sb = sb("proj_sb", [P, FCH, D])
        gate_sb = sb("gate_sb", [P, KC, EXPERTS])
        sgup_sb = sb("sgup_sb", [P, KC, 2 * HALF])
        sgdn_sb = sb("sgdn_sb", [P, HCH, D])
        exp_sb = sb("exp_sb", [P, EXPERTS, EXW])
        ln_sb = sb("ln_sb", [P, 4, KC])
        fcb_sb = sb("fcb_sb", [P, FCH])
        ones_bf = sb("ones_bf", [P, P], BF16)
        before_bf = sb("before_bf", [P, P], BF16)
        bias_bf = sb("bias_bf", [P, 5 * D], BF16)
        ident = sb("ident", [P, P])

        xin = sb("xin", [P, TPB, D])
        xnT = [sb(f"xnT{j}", [P, KC, P]) for j in range(2)]
        eqk = sb("eqk", [P, 2 * D])
        rqk = sb("rqk", [P, 2 * D])
        v_dve = [sb(f"v_dve{j}", [P, HD, HEADS]) for j in range(2)]
        v_pool = sb("v_pool", [P, HEADS, HE])
        fq = [sb(f"fq{j}", [P, HEADS, HD]) for j in range(2)]
        fqk_pool = sb("fqk_pool", [P, 2, HEADS, HD])
        prod = sb("prod", [P, HEADS * HE * HD])
        prod_pool = sb("prod_pool", [P, HEADS * HE * HD])
        qkv = [sb(f"qkv{j}", [P, HEADS, HE]) for j in range(2)]
        kvT_pool = sb("kvT_pool", [P, HE, HD])
        kv_pool = sb("kv_pool", [P, HD, HE])
        qkv_pool = sb("qkv_pool", [P, HEADS, HE])
        attn = sb("attn", [P, TPB, D])
        xres = sb("xres", [P, TPB, D])
        xmid = sb("xmid", [P, TPB, D])
        bT = sb("bT", [P, KC, BLOCK])
        hid = sb("hid", [P, FCH, BLOCK])
        x1 = sb("x1", [P, TPB, D])
        rows = sb("rows", [P, TPB, ROW])
        sg_g = hid[:, 0:HCH, :]
        sg_u = hid[:, HCH:2 * HCH, :]
        hnorm = hid[:, FCH - 2:FCH, :].rearrange("p a (t d) -> p (a t) d", d=D)
        st6 = sb("st6", [P, TPB, 6])
        mv_a = sb("mv_a", [P, TPB, 2])
        sq_a = sb("sq_a", [P, 2, TPB])
        rs_a = sb("rs_a", [P, 3, TPB])
        a_scale = sb("a_scale", [P, 2, TPB])
        mv_b = sb("mv_b", [P, TPB, 2])
        sq_b = sb("sq_b", [P, TPB])
        rs_b = sb("rs_b", [P, 2, TPB])
        den = sb("den", [P, HEADS])
        act_tmp = sb("act_tmp", [P, 2])
        top_v = sb("top_v", [P, TPB, 8])
        top_i = sb("top_i", [P, TPB, 8], UINT32)
        iota_e = sb("iota_e", [P, EXPERTS])
        iota_r = sb("iota_r", [P, EXPERTS])
        first2 = sb("first2", [P, 2, TPB])
        gap = sb("gap", [P, TPB])
        gap_e = sb("gap_e", [P, TPB])
        onehot = sb("onehot", [P, 2, TPB, EXPERTS])
        chosen = sb("chosen", [P, TPB, EXPERTS], BF16)
        free_row = sb("free_row", [P, EXPERTS])
        rank = sb("rank", [P, TPB, EXPERTS])
        slot_w = sb("slot_w", [P, 2, TPB, EXPERTS])
        slot = sb("slot", [P, 2 * TPB], INT32)
        tok = sb("tok", [P, TPB])
        pad_row = sb("pad_row", [P, ROW])
        pad_at = sb("pad_at", [P, EXPERTS], INT32)
        iota_p = sb("iota_p", [P, 1])
        tok_i = [sb(f"tok_i{j}", [P, 1], INT32) for j in range(2)]
        xg = [prod[:, j * ROW:(j + 1) * ROW] for j in range(2)]
        xgT = [prod[:, 1024 + j * D:1024 + (j + 1) * D] for j in range(2)]
        hg = prod[:, 2048:2048 + HALF]
        hact = prod[:, 2560:2560 + HALF]
        hgT = [prod[:, 3072 + j * HALF:3072 + (j + 1) * HALF] for j in range(2)]
        tab_e, tab_ei, tab_row = (prod[:, 3840 + i * SORTED_TILES:3840 + (i + 1) * SORTED_TILES]
                                  for i in range(3))
        tab_ei, tab_row = tab_ei.bitcast(INT32), tab_row.bitcast(INT32)
        w_row = [prod[:, 4280 + j:4281 + j] for j in range(2)]
        w_tmp = prod[:, 4288:4290]
        meta = prod[:, 4296:4300]
        tiles_f, tiles_to, cnt_i = (prod[:, 4248 + i * EXPERTS:4248 + (i + 1) * EXPERTS] for i in range(3))
        cnt_i = cnt_i.bitcast(INT32)
        tab_first = prod_pool[:, 0:SORTED_TILES]
        iota_k = prod_pool[:, 1024:1024 + SORTED_TILES]
        bias_hi = prod_pool[:, 0:5 * D // 2].bitcast(BF16)
        yg = [prod_pool[:, j * D:(j + 1) * D] for j in range(2)]

        def bank(name):
            return ctx.enter_context(nc.psum_tensor(name, [P, 512], FP32))
        p_xT, p_q0, p_q1, p_core, p_b0, p_b1, p_b2, p_b3 = (
            bank(n) for n in ("p_xT", "p_q0", "p_q1", "p_core", "p_b0", "p_b1", "p_b2", "p_b3"))
        shared_bank = (p_b0, p_b2, p_b3)
        LOGITS, RANKS = 0, 2 * TPB * EXPERTS
        gate_bank, up_bank, y_bank = (p_q0, p_b0), (p_q1, p_b1), (p_b2, p_b3)

        weights_in = [sem(f"weights_in{j}") for j in range(3)]
        experts_in = sem("experts_in")
        pool_const = sem("pool_const")
        const_ready = sem("const_ready")
        xin_loaded = sem("xin_loaded")
        ln1_var = sem("ln1_var")
        ln1_std = sem("ln1_std")
        ln1_scale = sem("ln1_scale")
        xhat_ready = sem("xhat_ready")
        scale_ready = sem("scale_ready")
        xT_psum = sem("xT_psum")
        xnT_ready = sem("xnT_ready")
        qkv_psum = sem("qkv_psum")
        qkv_taken = sem("qkv_taken")
        feat_ready = sem("feat_ready")
        pool_v_used = sem("pool_v_used")
        pool_qkv = sem("pool_qkv")
        share_ready = sem("share_ready")
        share_done = sem("share_done")
        attn_ready = sem("attn_ready")
        attnT_psum = sem("attnT_psum")
        attnT_ready = sem("attnT_ready")
        xres_loaded = sem("xres_loaded")
        a_ready = sem("a_ready")
        wo_psum = sem("wo_psum")
        ln2_var = sem("ln2_var")
        ln2_std = sem("ln2_std")
        ln2_scale = sem("ln2_scale")
        xsum_ready = sem("xsum_ready")
        h_ready = sem("h_ready")
        hT_psum = sem("hT_psum")
        hT_ready = sem("hT_ready")
        fc_psum = sem("fc_psum")
        gelu_ready = sem("gelu_ready")
        proj_psum = sem("proj_psum")
        x1_read = sem("x1_read")
        ln3_std = sem("ln3_std")
        ln3_scale = sem("ln3_scale")
        rows_ready = sem("rows_ready")
        x3T_psum = sem("x3T_psum")
        x3T_ready = sem("x3T_ready")
        logits_psum = sem("logits_psum")
        gap_ready = sem("gap_ready")
        gap_exp = sem("gap_exp")
        chosen_ready = sem("chosen_ready")
        ranks_psum = sem("ranks_psum")
        ranks_read = sem("ranks_read")
        slots_ready = sem("slots_ready")
        scattered = sem("scattered")
        up_psum = sem("up_psum")
        up_taken = sem("up_taken")
        shared_h = sem("shared_h")
        down_psum = sem("down_psum")
        out_ready = sem("out_ready")
        out_stored = sem("out_stored")
        dve_done = sem("dve_done")
        pool_done = sem("pool_done")
        init_stored = sem("init_stored")
        pads_at = sem("pads_at")
        pads_stored = sem("pads_stored")
        waits_passed = sem("waits_passed")
        tables_ready = sem("tables_ready")
        xg_loaded = [sem(f"xg_loaded{j}") for j in range(2)]
        xg_meta = sem("xg_meta")
        w_ready = sem("w_ready")
        gT_psum = sem("gT_psum")
        gT_ready = sem("gT_ready")
        gate_psum = sem("gate_psum")
        gu_psum = sem("gu_psum")
        g_act = sem("g_act")
        hg_ready = sem("hg_ready")
        hgT_psum = sem("hgT_psum")
        hgT_ready = sem("hgT_ready")
        y_psum = sem("y_psum")
        y_ready = sem("y_ready")
        added = sem("added")

        def wait(eng, s, value):
            if not isinstance(value, int) or value > 0:
                eng.wait_ge(s, value)

        def stand_alone(eng):
            eng.sem_inc(waits_passed, 1)

        class Chain:

            def __init__(self, eng, s):
                self.eng, self.s, self.base, self.n = eng, s, 0, 0

            def __call__(self, ins):
                self.later(ins)
                self.sync()

            def later(self, ins):
                self.n += 1
                ins.then_inc(self.s, 1)
                return self.n

            def reached(self, n):
                self.eng.wait_ge(self.s, self.base + n)

            def sync(self):
                self.eng.wait_ge(self.s, self.base + self.n)

            def enter(self, done, per_round):
                self.before, self.per_round = self.base + self.n, per_round
                self.base, self.n = self.before + done * per_round, 0

            def leave(self, rounds):
                assert self.n == self.per_round, f"{self.n} steps in a round"
                self.base, self.n = self.before + rounds * self.per_round, 0

        def announce(eng, ins, s, value):
            ins.then_inc(s, 1)
            eng.wait_ge(s, value)

        FIRST, LAST = 3, BLOCKS

        block = ctx.enter_context(nc.Block())

        @block.sync
        def _(sp):
            sp.dma_start(xin[:], x_blk[0]).then_inc(xin_loaded, 16)
            for dst, src in ((wqkv_sb, wqkv), (ln_sb[:, 0, :], ln1w), (ln_sb[:, 1, :], ln1b),
                             (ln_sb[:, 2, :], ln2w), (ln_sb[:, 3, :], ln2b), (fcb_sb, fc_b)):
                sp.dma_start(dst[:] if dst in (wqkv_sb, fcb_sb) else dst, src).then_inc(weights_in[0], 16)
            sp.dma_start(prod[:, 0:5 * D], b_tok.to_broadcast([P, 5 * D])).then_inc(weights_in[0], 16)
            for dst, src in ((wo_sb, wo), (fc_sb, fc_w), (proj_sb, proj_w)):
                sp.dma_start(dst[:], src).then_inc(weights_in[1], 16)
            for dst, src in ((gate_sb, gate_w), (sgup_sb, sg_up), (sgdn_sb, sg_down)):
                sp.dma_start(dst[:], src).then_inc(weights_in[2], 16)
            for e in range(EXPERTS):
                sp.dma_start(exp_sb[:, e, :], experts[e]).then_inc(experts_in, 16)

            sp.wait_ge(const_ready, 1)
            sp.dma_start(rows_sorted[EXPERTS * REGION:, :].rearrange("(j p) d -> p j d", p=P),
                         pad_row[:].unsqueeze(1).to_broadcast([P, SPARE_TILES, ROW])
                         ).then_inc(init_stored, 16)
            sp.dma_start(out[TOKENS:TOKENS + P, :], pad_row[:, 0:D]).then_inc(init_stored, 16)

            def body(c, core, stage_b, tail):
                if stage_b:
                    wait(sp, x1_read, c - 1)
                    sp.dma_start(xres[:], x_blk[bass.ds(c - 1, 1)].rearrange("b p t d -> p (b t) d")
                                 ).then_inc(xres_loaded, 16)
                if core and (not isinstance(c, int) or c < BLOCKS - 1):
                    wait(sp, xT_psum, 4 * (c + 1))
                    sp.dma_start(xin[:], x_blk[bass.ds(c + 1, 1)].rearrange("b p t d -> p (b t) d")
                                 ).then_inc(xin_loaded, 16)
                if tail:
                    wait(sp, out_ready, c - 1)
                    sp.dma_start(out_blk[bass.ds(c - 2, 1)].rearrange("b p t d -> p (b t) d"), x1[:]
                                 ).then_inc(out_stored, 16)

            for c in range(FIRST):
                body(c, True, c >= 1, c >= 2)
            with sp.Fori(FIRST, LAST - 1) as c:
                body(c, True, True, True)
            body(BLOCKS - 1, True, True, True)
            body(BLOCKS, False, True, True)
            body(BLOCKS + 1, False, False, True)

            sp.wait_ge(tables_ready, 1)
            sp.wait_ge(init_stored, 32)
            sp.wait_ge(pads_stored, 16 * EXPERTS)
            sp.wait_ge(scattered, 16 * 2 * TPB * BLOCKS)

            def load(k, j):
                row = sp.value_load(tab_row[0:1, bass.ds(k, 1)], min_val=0,
                                    max_val=EXPERTS * REGION + (SPARE_TILES - 1) * P)
                wait(sp, gT_psum, k - 1)
                wait(sp, xg_meta, k - 1)
                sp.dma_start(xg[j], rows_sorted[bass.ds(row, P), :]).then_inc(xg_loaded[j], 16)
            load(0, 0)
            load(1, 1)
            with sp.Fori(1, SORTED_TILES // 2) as m:
                load(2 * m, 0)
                load(2 * m + 1, 1)
            sp.wait_ge(out_stored, 16 * BLOCKS)
            sp.wait_ge(added, 16 * SORTED_TILES)

        @block.gpsimd
        def _(pool):
            g = nc.gpsimd
            done = Chain(pool, pool_done)
            done(g.memset(ident[:], 0.0))
            g.affine_select(out=ident[:], in_=ident[:], compare_op=ALU.not_equal, fill=1.0, base=0,
                            pattern=[[-1, P]], channel_multiplier=1).then_inc(pool_const, 1)
            done(g.memset(ones_bf[:], 1.0))
            g.affine_select(out=before_bf[:], in_=ones_bf[:], compare_op=ALU.is_gt, fill=0.0, base=0,
                            pattern=[[1, P]], channel_multiplier=-1).then_inc(pool_const, 1)
            done(g.memset(v_pool[:], 1.0))
            g.iota(iota_e[:], [[1, EXPERTS]], base=0, channel_multiplier=0,
                   allow_small_or_imprecise_dtypes=True).then_inc(pool_const, 1)
            g.iota(iota_r[:], [[REGION, EXPERTS]], base=0, channel_multiplier=0,
                   allow_small_or_imprecise_dtypes=True).then_inc(pool_const, 1)
            g.iota(tok[:], [[P, TPB]], base=-BLOCK, channel_multiplier=1,
                   allow_small_or_imprecise_dtypes=True).then_inc(pool_const, 1)
            g.iota(iota_p[:], [[0, 1]], base=0, channel_multiplier=1,
                   allow_small_or_imprecise_dtypes=True).then_inc(pool_const, 1)

            def halve(dst):
                w = dst.shape[-1]
                for n in (8, 4, 2):
                    done(g.tensor_tensor(prod_pool[:, 0:n * w], prod_pool[:, 0:n * w],
                                         prod_pool[:, n * w:2 * n * w], ALU.add))
                return g.tensor_tensor(dst, prod_pool[:, 0:w], prod_pool[:, w:2 * w], ALU.add)

            def heads(c, u):
                wait(pool, share_ready, 3 * c + u)
                done(g.tensor_tensor(
                    prod_pool[:, 0:HD * POOL_HEADS * HE].rearrange("p (d h e) -> p d h e", d=HD, e=HE),
                    fq[u % 2][:, DVE_HEADS:, :].rearrange("p h d -> p d h").unsqueeze(3)
                    .to_broadcast([P, HD, POOL_HEADS, HE]),
                    kvT_pool[:].rearrange("p e d -> p d e").unsqueeze(2)
                    .to_broadcast([P, HD, POOL_HEADS, HE]), ALU.mult))
                announce(pool, halve(qkv[u % 2][:, DVE_HEADS:, :].rearrange("p h e -> p (h e)")),
                         share_done, 3 * c + u)

            def scatter(c):
                wait(pool, slots_ready, c - 1)
                stand_alone(pool)
                done.later(g.tensor_scalar(tok[:], tok[:], float(BLOCK), None, ALU.add))
                done(g.tensor_copy(rows[:, :, C_E0], first2[:, 0, :]))
                stand_alone(pool)
                done(g.tensor_copy(rows[:, :, C_TOK], tok[:]))
                stand_alone(pool)
                for s in range(2):
                    for t in range(TPB):
                        pool.indirect_dma_start(
                            out=rows_sorted[:, :],
                            out_offset=bass.IndirectOffsetOnAxis(
                                ap=slot[:, s * TPB + t:s * TPB + t + 1], axis=0),
                            in_=rows[:, t, :], in_offset=None).then_inc(scattered, 16)

            def gate_shared(c):
                wait(pool, up_taken, 2 * HCH * (c - 1))
                announce(pool, g.tensor_tensor(sg_g, sg_g, sg_u, ALU.mult), shared_h, c - 1)

            def body(c, core, stage_b, tail):
                if tail and core:
                    scatter(c)
                    gate_shared(c)
                elif tail:
                    gate_shared(c)
                    scatter(c)
                if core:
                    wait(pool, feat_ready, 4 * c + 1)
                    done(g.tensor_tensor(
                        prod_pool[:].rearrange("p (h d e) -> p h d e", h=HEADS, d=HD),
                        fqk_pool[:, 1].unsqueeze(3).to_broadcast([P, HEADS, HD, HE]),
                        v_pool[:].unsqueeze(2).to_broadcast([P, HEADS, HD, HE]), ALU.mult))
                    announce(pool, halve(kv_pool[:].rearrange("p d e -> p (d e)")), pool_v_used, c + 1)
                    heads(c, 1)
                if stage_b:
                    wait(pool, xres_loaded, 16 * c)
                    wait(pool, ln2_var, c)
                    announce(pool, g.tensor_tensor(xres[:], xres[:], xmid[:], ALU.add), xsum_ready, c)
                if core:
                    heads(c, 2)
                    done(g.tensor_tensor(
                        prod_pool[:].rearrange("p (d h e) -> p d h e", d=HD, h=HEADS),
                        fqk_pool[:, 0].rearrange("p h d -> p d h").unsqueeze(3)
                        .to_broadcast([P, HD, HEADS, HE]),
                        kv_pool[:].unsqueeze(2).to_broadcast([P, HD, HEADS, HE]), ALU.mult))
                    announce(pool, halve(qkv_pool[:].rearrange("p h e -> p (h e)")), pool_qkv, c + 1)
                    heads(c, 3)

            for c in range(FIRST):
                body(c, True, c >= 1, c >= 2)
            with pool.Fori(FIRST, LAST) as c:
                done.enter(c - FIRST, POOL_STEPS)
                body(c, True, True, True)
                done.leave(LAST - FIRST)
            body(BLOCKS, False, True, True)
            g.iota(iota_k, [[1, SORTED_TILES]], base=0, channel_multiplier=0,
                   allow_small_or_imprecise_dtypes=True).then_inc(pool_const, 1)
            body(BLOCKS + 1, False, False, True)

            pool.wait_ge(pads_at, 1)
            for e in range(EXPERTS):
                pool.indirect_dma_start(out=rows_sorted[:, :],
                                        out_offset=bass.IndirectOffsetOnAxis(ap=pad_at[:, e:e + 1], axis=0),
                                        in_=pad_row[:], in_offset=None).then_inc(pads_stored, 16)

            pool.wait_ge(out_stored, 16 * BLOCKS)
            pool.wait_ge(init_stored, 32)

            def add(k, j):
                pool.wait_ge(y_ready, k + 1)
                wait(pool, added, 16 * k)
                stand_alone(pool)
                pool.indirect_dma_start(out=out[:, :],
                                        out_offset=bass.IndirectOffsetOnAxis(ap=tok_i[j][:], axis=0),
                                        in_=yg[j], in_offset=None, compute_op=ALU.add).then_inc(added, 16)
            add(0, 0)
            add(1, 1)
            with pool.Fori(1, SORTED_TILES // 2) as m:
                add(2 * m, 0)
                add(2 * m + 1, 1)

        @block.scalar
        def _(act):
            a = nc.scalar

            def take_x(c, u):
                n = 4 * c + u
                wait(act, xT_psum, n + 1)
                wait(act, qkv_psum, n - 1)
                for k in range(KC):
                    ins = a.activation(xnT[u % 2][:, k, :], p_xT[:, k * P:(k + 1) * P], ACT.Identity,
                                       bias=ln_sb[:, 1, k:k + 1], scale=ln_sb[:, 0, k:k + 1])
                ins.then_inc(xnT_ready, 1)

            def take_qkv(c, u):
                n = 4 * c + u
                wait(act, qkv_psum, n + 1)
                wait(act, feat_ready, n)
                a.activation(eqk[:], p_q0[:], ACT.Exp)
                a.activation(rqk[:], p_q0[:], ACT.Relu)
                v = p_q1[:, 0:D].rearrange("p (h e) -> p h e", h=HEADS)
                if u == 0:
                    wait(act, pool_v_used, c)
                    ins = a.activation(v_pool[:, :, 0:HD], v, ACT.Copy)
                else:
                    ins = a.activation(v_dve[u % 2][:].rearrange("p e h -> p h e"), v, ACT.Copy)
                ins.then_inc(qkv_taken, 1)

            def norm(dst, src, scales, ready):
                for t in range(TPB):
                    a.activation(dst(t), src(t), ACT.Identity, bias=scales[:, 1, t:t + 1],
                                 scale=scales[:, 0, t:t + 1]).then_inc(ready, 1)

            def norm_1(b):
                wait(act, ln1_scale, b + 1)
                norm(lambda t: xin[:, t, :], lambda t: xin[:, t, :], rs_a[:, 1:3], xhat_ready)

            def take_pair(c, banks, psum, ready):
                for k, bnk in enumerate(banks):
                    wait(act, psum, KC * (c - 1) + k + 1)
                    a.activation(bT[:, k, :], bnk[:], ACT.Copy).then_inc(ready, 1)

            def table(func):
                a.activation(act_tmp[:, 1:2], act_tmp[:, 0:1], func)

            def body(c, core, stage_b, tail):
                more = core and (not isinstance(c, int) or c < BLOCKS - 1)
                if core:
                    take_x(c, 2)
                if stage_b:
                    take_pair(c, (p_b0, p_b1), attnT_psum, attnT_ready)
                if core:
                    take_x(c, 3)
                if stage_b:
                    wait(act, xres_loaded, 16 * c)
                    wait(act, scale_ready, c)
                    wait(act, xsum_ready, c - 1)
                    norm(lambda t: xmid[:, t, :], lambda t: xres[:, t, :], a_scale, a_ready)
                if stage_b:
                    table(ACT.Sqrt)
                    wait(act, ln2_var, c)
                    a.activation(sq_b[:], sq_b[:], ACT.Sqrt).then_inc(ln2_std, 1)
                    wait(act, ln2_scale, c)
                    wait(act, proj_psum, c - 1)
                    norm(lambda t: hnorm[:, t, :], lambda t: xmid[:, t, :], rs_b, h_ready)
                if more:
                    wait(act, ln1_var, c + 2)
                    a.activation(sq_a[:], sq_a[:], ACT.Sqrt).then_inc(ln1_std, 1)
                if core:
                    take_qkv(c, 2)
                if stage_b:
                    for k, bnk in enumerate((p_b2, p_b3)):
                        wait(act, hT_psum, KC * (c - 1) + k + 1)
                        a.activation(bT[:, k, :], bnk[:], ACT.Identity, bias=ln_sb[:, 3, k:k + 1],
                                     scale=ln_sb[:, 2, k:k + 1]).then_inc(hT_ready, 1)
                    table(ACT.Gelu)
                    for f in range(FCH):
                        wait(act, fc_psum, FCH * (c - 1) + f + 1)
                        if f == 0:
                            wait(act, down_psum, c - 2)
                        a.activation(hid[:, f, :], (p_b2, p_b3)[f % 2][:], ACT.Gelu,
                                     bias=fcb_sb[:, f:f + 1]).then_inc(gelu_ready, 1)
                if core:
                    take_qkv(c, 3)
                if more:
                    norm_1(c + 1)
                    take_x(c + 1, 0)
                    take_x(c + 1, 1)
                    take_qkv(c + 1, 0)
                if stage_b:
                    table(ACT.Sqrt)
                    wait(act, x1_read, c)
                    a.activation(sq_b[:], sq_b[:], ACT.Sqrt).then_inc(ln3_std, 1)
                    wait(act, ln3_scale, c)
                    wait(act, scattered, 16 * 2 * TPB * (c - 1))
                    norm(lambda t: rows[:, t, 0:D], lambda t: x1[:, t, :], rs_b, rows_ready)
                    take_pair(c, (p_b2, p_b3), x3T_psum, x3T_ready)
                if more:
                    take_qkv(c + 1, 1)
                if stage_b:
                    wait(act, gap_ready, c)
                    a.activation(gap_e[:], gap[:], ACT.Exp).then_inc(gap_exp, 1)
                    table(ACT.Silu)
                    for n in range(2 * HCH):
                        wait(act, up_psum, 2 * HCH * (c - 1) + n + 1)
                        dst, func = ((sg_g, ACT.Silu), (sg_u, ACT.Copy))[n % 2]
                        a.activation(dst[:, n // 2, :], shared_bank[n % 3][:], func).then_inc(up_taken, 1)

            act.wait_ge(weights_in[0], 16 * 7)
            act.wait_ge(pool_const, 3)
            act.wait_ge(const_ready, 1)
            wait(act, ln1_var, 1)
            a.activation(sq_a[:], sq_a[:], ACT.Sqrt).then_inc(ln1_std, 1)
            norm_1(0)
            take_x(0, 0)
            take_x(0, 1)
            take_qkv(0, 0)
            take_qkv(0, 1)
            for c in range(FIRST):
                body(c, True, c >= 1, c >= 2)
            with act.Fori(FIRST, LAST - 1) as c:
                body(c, True, True, True)
            body(BLOCKS - 1, True, True, True)
            body(BLOCKS, False, True, True)

            def take_gT(k, j):
                act.wait_ge(gT_psum, k + 1)
                wait(act, gu_psum, k - 1)
                a.activation(xgT[j], p_xT[:, 0:D], ACT.Copy).then_inc(gT_ready, 1)

            def silu(k, j):
                act.wait_ge(gate_psum, k + 1)
                wait(act, hg_ready, k)
                a.activation(hact, gate_bank[j][:, 0:HALF], ACT.Silu).then_inc(g_act, 1)

            def weigh(k, j):
                act.wait_ge(y_psum, k + 1)
                wait(act, w_ready, k + 1)
                wait(act, added, 16 * (k - 1))
                a.activation(yg[j], y_bank[j][:, 0:D], ACT.Copy, scale=w_row[j]).then_inc(y_ready, 1)

            act.wait_ge(tables_ready, 1)
            take_gT(0, 0)
            silu(0, 0)
            take_gT(1, 1)

            def pair(k, j):
                silu(k, j)
                take_gT(k + 1, 1 - j)
                weigh(k - 1, 1 - j)
            pair(1, 1)
            pair(2, 0)
            with act.Fori(1, (SORTED_TILES - 2) // 2) as m:
                pair(2 * m + 1, 1)
                pair(2 * m + 2, 0)
            silu(SORTED_TILES - 1, 1)
            weigh(SORTED_TILES - 2, 0)
            weigh(SORTED_TILES - 1, 1)

        @block.vector
        def _(dve):
            v = nc.vector
            done = Chain(dve, dve_done)

            def stats(src, mv):
                for t in range(TPB):
                    done.later(v.bn_stats(st6[:, t, :], src(t)))
                done.sync()
                stand_alone(dve)
                for t in range(TPB):
                    done.later(v.bn_aggr(mv[:, t, :], st6[:, t, :]))
                done.sync()

            def ln1_stats(b):
                wait(dve, xin_loaded, 16 * (b + 1))
                stats(lambda t: xin[:, t, :], mv_a)
                done.later(v.tensor_scalar(sq_a[:, 0, :], mv_a[:, :, 1], 1.0, EPS, ALU.mult, ALU.add))
                announce(dve, v.tensor_scalar(sq_a[:, 1, :], mv_a[:, :, 1], 1.0 + EPS, EPS * EPS,
                                              ALU.mult, ALU.add), ln1_var, b + 1)

            def ln1_scales(b):
                wait(dve, ln1_std, b + 1)
                done(v.reciprocal(rs_a[:, 0:2], sq_a[:]))
                announce(dve, v.scalar_tensor_tensor(rs_a[:, 2, :], mv_a[:, :, 0], -1.0, rs_a[:, 1, :],
                                                     ALU.mult, ALU.mult), ln1_scale, b + 1)

            def scales_b(std, scale, c):
                wait(dve, std, c)
                done(v.reciprocal(rs_b[:, 0], sq_b[:]))
                announce(dve, v.scalar_tensor_tensor(rs_b[:, 1, :], mv_b[:, :, 0], -1.0, rs_b[:, 0, :],
                                                     ALU.mult, ALU.mult), scale, c)

            def keep_scales(c):
                wait(dve, a_ready, TPB * c)
                done.later(v.tensor_copy(a_scale[:, 0, :], rs_a[:, 0, :]))
                announce(dve, v.scalar_tensor_tensor(a_scale[:, 1, :], mv_a[:, :, 0], -1.0, rs_a[:, 0, :],
                                                     ALU.mult, ALU.mult), scale_ready, c + 1)

            def features(c, u):
                n = 4 * c + u
                wait(dve, qkv_taken, n + 1)
                if u == 0:
                    ins = v.scalar_tensor_tensor(fqk_pool[:].rearrange("p a h d -> p (a h d)"), eqk[:], 1.0,
                                                 rqk[:], ALU.min, ALU.add)
                else:
                    done.later(v.scalar_tensor_tensor(fq[u % 2][:].rearrange("p h d -> p (h d)"), eqk[:, 0:D], 1.0,
                                                      rqk[:, 0:D], ALU.min, ALU.add))
                    ins = v.scalar_tensor_tensor(
                        fkT, eqk[:, D:2 * D].rearrange("p (h d) -> p d h", h=HEADS), 1.0,
                        rqk[:, D:2 * D].rearrange("p (h d) -> p d h", h=HEADS), ALU.min, ALU.add)
                announce(dve, ins, feat_ready, n + 1)

            fkT = p_core[:, 0:D].rearrange("p (d h) -> p d h", d=HD)
            kv_first = 512 - HE * HD
            kvT = p_core[:, kv_first:512].rearrange("p (e d) -> p e d", e=HE)

            def kv_products(u):
                done.later(v.tensor_reduce(kvT[:, HD, :], fkT, AX.X, ALU.add))
                done.later(v.tensor_tensor(
                    prod[:, 0:HD * HD * HEADS].rearrange("p (e d h) -> p e d h", e=HD, d=HD),
                    fkT.unsqueeze(1).to_broadcast([P, HD, HD, HEADS]),
                    v_dve[u % 2][:].unsqueeze(2).to_broadcast([P, HD, HD, HEADS]), ALU.mult))

            def kv_sums(half):
                n = HD * HD // 2
                done.later(v.tensor_reduce(
                    p_core[:, kv_first + half * n:kv_first + (half + 1) * n],
                    prod[:, half * n * HEADS:(half + 1) * n * HEADS].rearrange("p (a h) -> p a h", h=HEADS),
                    AX.X, ALU.add))

            def share(c, u):
                done.sync()
                announce(dve, v.tensor_copy(kvT_pool[:], kvT), share_ready, 3 * c + u)

            def q_products(u):
                done.sync()
                done.later(v.tensor_tensor(
                    prod[:, 0:DVE_HEADS * HE * HD].rearrange("p (h e d) -> p h e d", h=DVE_HEADS, e=HE),
                    fq[u % 2][:, 0:DVE_HEADS].unsqueeze(2).to_broadcast([P, DVE_HEADS, HE, HD]),
                    kvT.unsqueeze(1).to_broadcast([P, DVE_HEADS, HE, HD]), ALU.mult))

            def q_sums(u):
                done.sync()
                done.later(v.tensor_reduce(
                    qkv[u % 2][:, 0:DVE_HEADS].rearrange("p h e -> p (h e)"),
                    prod[:, 0:DVE_HEADS * HE * HD].rearrange("p (a d) -> p a d", d=HD), AX.X, ALU.add))

            def divide_1(src):
                return done.later(v.tensor_scalar(den[:], src[:, :, HD], 1e-6, None, ALU.add))

            def divide_2(first):
                done.reached(first)
                return done.later(v.reciprocal(den[:], den[:]))

            def divide_3(second, c, t, src):
                done.reached(second)
                return v.tensor_tensor(attn[:, t, :].rearrange("p (h e) -> p h e", h=HEADS),
                                       src[:, :, 0:HD], den[:].unsqueeze(2).to_broadcast([P, HEADS, HD]),
                                       ALU.mult)

            def divide_and_sum(c, u):
                done.sync()
                src = qkv[(u - 1) % 2]
                wait(dve, share_done, 3 * c + u - 1)
                wait(dve, attnT_psum, KC * c)
                first = divide_1(src)
                kv_sums(0)
                second = divide_2(first)
                kv_sums(1)
                done.later(divide_3(second, c, u - 2, src))

            def residual_1(c):
                wait(dve, a_ready, TPB * c)
                wait(dve, wo_psum, c)
                flat = xmid[:].rearrange("p t d -> p (t d)")
                for k, bnk in enumerate((p_b2, p_b3)):
                    done.later(v.tensor_tensor(flat[:, 512 * k:512 * k + 512],
                                               flat[:, 512 * k:512 * k + 512], bnk[:], ALU.add))
                done.sync()
                stats(lambda t: xmid[:, t, :], mv_b)
                announce(dve, v.tensor_scalar(sq_b[:], mv_b[:, :, 1], 1.0, EPS, ALU.mult, ALU.add),
                         ln2_var, c)

            def residual_2(c):
                wait(dve, proj_psum, c)
                wait(dve, xsum_ready, c)
                wait(dve, out_stored, 16 * (c - 1))
                flat, res = (z[:].rearrange("p t d -> p (t d)") for z in (x1, xres))
                for k, bnk in enumerate((p_b0, p_b1)):
                    done.later(v.tensor_tensor(flat[:, 512 * k:512 * k + 512],
                                               res[:, 512 * k:512 * k + 512], bnk[:], ALU.add))
                done.sync()
                stats(lambda t: x1[:, t, :], mv_b)
                announce(dve, v.tensor_scalar(sq_b[:], mv_b[:, :, 1], 1.0, EPS, ALU.mult, ALU.add),
                         x1_read, c)

            def choose(c):
                wait(dve, logits_psum, c)
                stand_alone(dve)
                logit = [p_b1[:, LOGITS + t * EXPERTS:LOGITS + (t + 1) * EXPERTS] for t in range(TPB)]
                for t in range(TPB):
                    done.later(v.max(top_v[:, t, :], logit[t]))
                done.sync()
                stand_alone(dve)
                for t in range(TPB):
                    done.later(v.max_index(top_i[:, t, :], top_v[:, t, :], logit[t]))
                announce(dve, v.tensor_tensor(gap[:], top_v[:, :, 1], top_v[:, :, 0], ALU.subtract),
                         gap_ready, c)
                wait(dve, scattered, 16 * 2 * TPB * (c - 1))
                done.sync()
                done(v.tensor_copy(first2[:], top_i[:, :, 0:2].rearrange("p t s -> p s t")))
                for s in range(2):
                    done.later(v.tensor_tensor(
                        onehot[:, s], iota_e[:].unsqueeze(1).to_broadcast([P, TPB, EXPERTS]),
                        first2[:, s, :].unsqueeze(2).to_broadcast([P, TPB, EXPERTS]), ALU.is_equal))
                done.sync()
                announce(dve, v.tensor_tensor(chosen[:], onehot[:, 0], onehot[:, 1], ALU.add),
                         chosen_ready, c)

            def place(c):
                n = TPB * EXPERTS
                wait(dve, ranks_psum, c)
                done.later(v.tensor_tensor(
                    rank[:], p_b1[:, RANKS:RANKS + n].rearrange("p (t e) -> p t e", t=TPB),
                    free_row[:].unsqueeze(1).to_broadcast([P, TPB, EXPERTS]), ALU.add))
                done.sync()
                done.later(v.tensor_tensor(
                    slot_w[:].rearrange("p s t e -> p s (t e)"),
                    onehot[:].rearrange("p s t e -> p s (t e)"),
                    rank[:].rearrange("p t e -> p (t e)").unsqueeze(1).to_broadcast([P, 2, n]), ALU.mult))
                announce(dve, v.tensor_tensor(free_row[:], free_row[:], p_b1[:, RANKS + n:RANKS + n + EXPERTS],
                                              ALU.add), ranks_read, c)
                done.sync()
                with nc.allow_low_precision(reason="row numbers are whole and below 2^24"):
                    done.later(v.tensor_reduce(slot[:], slot_w[:].rearrange("p s t e -> p (s t) e"),
                                               AX.X, ALU.add))

            def weights(c):
                wait(dve, gap_exp, c)
                done(v.tensor_scalar(gap[:], gap_e[:], 1.0, None, ALU.add))
                done(v.reciprocal(rows[:, :, C_W0], gap[:]))
                announce(dve, v.tensor_tensor(rows[:, :, C_W1], gap_e[:], rows[:, :, C_W0], ALU.mult),
                         slots_ready, c)

            def finish(c):
                wait(dve, down_psum, c - 1)
                flat = x1[:].rearrange("p t d -> p (t d)")
                done.later(v.tensor_tensor(flat[:, 0:512], flat[:, 0:512], p_b0[:], ALU.add))
                announce(dve, v.tensor_tensor(flat[:, 512:1024], flat[:, 512:1024], p_b1[:], ALU.add),
                         out_ready, c - 1)

            def body(c, core, stage_b, tail):
                last = isinstance(c, int) and c >= BLOCKS - 1
                if core:
                    features(c, 1)
                    kv_products(1)
                if stage_b:
                    residual_1(c)
                if core:
                    keep_scales(c)
                if stage_b:
                    scales_b(ln2_std, ln2_scale, c)
                if core:
                    if not last:
                        ln1_stats(c + 1)
                    done.sync()
                    kv_sums(0)
                    kv_sums(1)
                    share(c, 1)
                    q_products(1)
                    if not last:
                        ln1_scales(c + 1)
                    q_sums(1)
                    features(c, 2)
                    kv_products(2)
                if tail:
                    finish(c)
                if core:
                    divide_and_sum(c, 2)
                    share(c, 2)
                    q_products(2)
                    q_sums(2)
                    features(c, 3)
                    kv_products(3)
                if stage_b:
                    residual_2(c)
                    scales_b(ln3_std, ln3_scale, c)
                if core:
                    divide_and_sum(c, 3)
                    share(c, 3)
                    q_products(3)
                    if not last:
                        wait(dve, pool_qkv, c + 1)
                        features(c + 1, 0)
                if stage_b:
                    choose(c)
                if core:
                    q_sums(3)
                    wait(dve, pool_qkv, c + 1)
                    second = divide_2(divide_1(qkv_pool))
                    wait(dve, attnT_psum, KC * c)
                    done(divide_3(second, c, POOL_TILE, qkv_pool))
                    wait(dve, share_done, 3 * c + 3)
                    second = divide_2(divide_1(qkv[1]))
                    announce(dve, divide_3(second, c, 2, qkv[1]), attn_ready, c + 1)
                if stage_b:
                    place(c)
                    weights(c)

            dve.wait_ge(weights_in[0], 16 * 7)
            dve.wait_ge(pool_const, 6)
            left = prod[:, 0:5 * D]
            part = prod[:, 5 * D:10 * D]
            done(v.memset(bias_bf[:], 0.0))
            for row in (0, 32, 64):
                done(v.tensor_copy(bias_bf[row:row + 1, :], left[row:row + 1, :]))
                if row < 64:
                    done(v.tensor_copy(bias_hi, left))
                    done(v.tensor_copy(part, bias_hi))
                    done(v.tensor_tensor(left, left, part, ALU.subtract))
            done(v.tensor_copy(free_row[:], iota_r[:]))
            done(v.memset(pad_row[:], 0.0))
            done(v.tensor_scalar(pad_row[:, C_TOK:C_TOK + 1], iota_p[:], float(TOKENS), None, ALU.add))
            announce(dve, v.memset(act_tmp[:], 0.0), const_ready, 1)
            ln1_stats(0)
            ln1_scales(0)
            features(0, 0)

            for c in range(FIRST):
                body(c, True, c >= 1, c >= 2)
            with dve.Fori(FIRST, LAST - 1) as c:
                done.enter(c - FIRST, DVE_STEPS)
                body(c, True, True, True)
                done.leave(LAST - 1 - FIRST)
            body(BLOCKS - 1, True, True, True)
            body(BLOCKS, False, True, True)
            announce(dve, v.tensor_scalar(pad_at[:], free_row[:], iota_p[:, 0:1], None, ALU.add), pads_at, 1)
            done(v.tensor_tensor(tiles_f, free_row[:], iota_r[:], ALU.subtract))
            done(v.tensor_scalar(cnt_i, tiles_f, float(P - 1), None, ALU.add))
            done(v.tensor_scalar(cnt_i, cnt_i, P.bit_length() - 1, None, ALU.arith_shift_right))
            done(v.tensor_copy(tiles_f, cnt_i))
            done(v.tensor_copy(tiles_to, tiles_f))
            for e in range(1, EXPERTS):
                done(v.tensor_tensor(tiles_to[:, e:e + 1], tiles_to[:, e:e + 1], tiles_to[:, e - 1:e], ALU.add))
            over = prod[:, 0:SORTED_TILES * EXPERTS].rearrange("p (k e) -> p k e", e=EXPERTS)
            wide = [P, SORTED_TILES, EXPERTS]
            dve.wait_ge(pool_const, 7)
            done(v.tensor_tensor(over, iota_k.unsqueeze(2).to_broadcast(wide),
                                 tiles_to.unsqueeze(1).to_broadcast(wide), ALU.is_ge))
            done(v.tensor_reduce(tab_e, over, AX.X, ALU.add))
            done(v.tensor_scalar(tab_ei, tab_e, float(EXPERTS - 1), None, ALU.min))
            done(v.tensor_tensor(over, over, tiles_f.unsqueeze(1).to_broadcast(wide), ALU.mult))
            done(v.tensor_reduce(tab_first, over, AX.X, ALU.add))
            done(v.tensor_tensor(tab_first, iota_k, tab_first, ALU.subtract))
            done(v.tensor_scalar(tab_first, tab_first, float(P), None, ALU.mult))
            announce(dve, v.scalar_tensor_tensor(tab_row, tab_e, float(REGION), tab_first,
                                                 ALU.mult, ALU.add), tables_ready, 1)
            body(BLOCKS + 1, False, False, True)

            def keep_meta(k, j):
                dve.wait_ge(xg_loaded[j], 16 * (k // 2 + 1) if isinstance(k, int) else 8 * (k - j) + 16)
                announce(dve, v.tensor_copy(meta, xg[j][:, D:ROW]), xg_meta, k + 1)

            def meta_weights(k, j):
                wait(dve, added, 16 * (k - 1))
                tok_c, w0, w1, e0 = (meta[:, i - D:i - D + 1] for i in (C_TOK, C_W0, C_W1, C_E0))
                done.later(v.tensor_copy(tok_i[j][:], tok_c))
                done(v.tensor_tensor(w_tmp[:, 0:1], e0, tab_e[:, bass.ds(k, 1)], ALU.is_equal))
                done(v.scalar_tensor_tensor(w_tmp[:, 1:2], w_tmp[:, 0:1], 0.0, w1, ALU.is_equal, ALU.mult))
                announce(dve, v.scalar_tensor_tensor(w_row[j], w0, w_tmp[:, 0:1], w_tmp[:, 1:2],
                                                     ALU.mult, ALU.add), w_ready, k + 1)

            def gated(k, j):
                dve.wait_ge(g_act, k + 1)
                dve.wait_ge(gu_psum, k + 1)
                wait(dve, hgT_psum, k)
                announce(dve, v.tensor_tensor(hg, hact, up_bank[j][:, 0:HALF], ALU.mult), hg_ready, k + 1)

            def take_hT(k, j):
                dve.wait_ge(hgT_psum, k + 1)
                wait(dve, y_psum, k - 1)
                announce(dve, v.tensor_copy(hgT[j], p_core[:, 0:HALF]), hgT_ready, k + 1)

            def tile(k, j):
                keep_meta(k, j)
                gated(k, j)
                take_hT(k, j)
                meta_weights(k, j)
            tile(0, 0)
            tile(1, 1)
            with dve.Fori(1, SORTED_TILES // 2) as m:
                done.enter(m - 1, 6)
                tile(2 * m, 0)
                tile(2 * m + 1, 1)
                done.leave(SORTED_TILES // 2 - 1)

        @block.tensor
        def _(pe):
            t_ = nc.tensor

            def project_x(c, u, part):
                n = 4 * c + u
                if part == "T":
                    wait(pe, xhat_ready, TPB * (c + 1))
                    wait(pe, xnT_ready, n)
                    for k in range(KC):
                        ins = t_.transpose(p_xT[:, k * P:(k + 1) * P],
                                           xin[:, ORDER[u], k * P:(k + 1) * P], ident[:])
                    ins.then_inc(xT_psum, 1)
                else:
                    wait(pe, xnT_ready, n + 1)
                    wait(pe, qkv_taken, n)
                    for bnk, lo, hi in ((p_q0, 0, 512), (p_q1, 512, 768)):
                        for k in range(KC):
                            t_.matmul(bnk[:, 0:hi - lo], xnT[u % 2][:, k, :], wqkv_sb[:, k, lo:hi],
                                      start=k == 0, stop=False)
                        ins = t_.matmul(bnk[:, 0:hi - lo], ones_bf[:], bias_bf[:, lo:hi],
                                        start=False, stop=True)
                    ins.then_inc(qkv_psum, 1)

            def transpose_block(src, banks, ready, tile_ready=None):
                for t in range(TPB):
                    if tile_ready:
                        tile_ready(t)
                    for k, bnk in enumerate(banks):
                        ins = t_.transpose(bnk[:, t * P:(t + 1) * P], src[:, t, k * P:(k + 1) * P], ident[:])
                        if t == TPB - 1:
                            ins.then_inc(ready, 1)

            def to_tokens(src, chunks, w, banks, bias_at, ready, at_last_chunk=None, between=None):
                for t in range(TPB):
                    o = banks[t // 2][:, (t % 2) * D:(t % 2 + 1) * D]
                    if t >= 2 and between:
                        between(t - 2)
                    for k in range(chunks):
                        if t == 0 and k == chunks - 1 and at_last_chunk:
                            at_last_chunk()
                        ins = t_.matmul(o, src[:, k, t * P:(t + 1) * P], w[:, k, :], start=k == 0,
                                        stop=bias_at is None and k == chunks - 1)
                    if bias_at is not None:
                        ins = t_.matmul(o, ones_bf[:], bias_bf[:, bias_at:bias_at + D], start=False, stop=True)
                ins.then_inc(ready, 1)

            def body(c, core, stage_b, tail):
                more = core and (not isinstance(c, int) or c < BLOCKS - 1)
                if core:
                    project_x(c, 2, "T")
                if stage_b:
                    wait(pe, attn_ready, c)
                    wait(pe, ranks_read, c - 1)
                    wait(pe, up_taken, 2 * HCH * (c - 1) - 2)
                    transpose_block(attn, (p_b0, p_b1), attnT_psum)
                if core:
                    project_x(c, 3, "T")
                if stage_b:
                    wait(pe, up_taken, 2 * HCH * (c - 1))
                    wait(pe, attnT_ready, KC * (c - 1) + 1)
                    to_tokens(bT, KC, wo_sb, (p_b2, p_b3), 3 * D, wo_psum,
                              at_last_chunk=lambda: wait(pe, attnT_ready, KC * c))
                if core:
                    project_x(c, 2, "P")
                if tail:
                    wait(pe, shared_h, c - 1)
                    if not stage_b:
                        wait(pe, ranks_read, c - 1)
                    to_tokens(sg_g, HCH, sgdn_sb, (p_b0, p_b1), None, down_psum)
                if stage_b:
                    transpose_block(hnorm, (p_b2, p_b3), hT_psum,
                                    lambda t: wait(pe, h_ready, TPB * (c - 1) + t + 1))
                if core:
                    project_x(c, 3, "P")
                if stage_b:
                    wait(pe, hT_ready, KC * (c - 1) + 1)
                    for f in range(FCH):
                        if f >= 2:
                            wait(pe, gelu_ready, FCH * (c - 1) + f - 1)
                        bnk = (p_b2, p_b3)[f % 2]
                        for k in range(KC):
                            if f == 0 and k == KC - 1:
                                wait(pe, hT_ready, KC * c)
                            ins = t_.matmul(bnk[:], fc_sb[:, k, f * P:(f + 1) * P], bT[:, k, :],
                                            start=k == 0, stop=k == KC - 1)
                        ins.then_inc(fc_psum, 1)
                    wait(pe, gelu_ready, FCH * c - 1)
                    wait(pe, out_ready, c - 1)
                    to_tokens(hid, FCH, proj_sb, (p_b0, p_b1), 4 * D, proj_psum,
                              at_last_chunk=lambda: wait(pe, gelu_ready, FCH * c),
                              between=(lambda u: project_x(c + 1, u, "T")) if more else None)
                elif more:
                    project_x(c + 1, 0, "T")
                    project_x(c + 1, 1, "T")
                if more:
                    project_x(c + 1, 0, "P")
                    project_x(c + 1, 1, "P")
                if stage_b:
                    transpose_block(rows, (p_b2, p_b3), x3T_psum,
                                    lambda t: wait(pe, rows_ready, TPB * (c - 1) + t + 1))
                    wait(pe, x3T_ready, KC * c)
                    for t in range(TPB):
                        for k in range(KC):
                            at = LOGITS + t * EXPERTS
                            ins = t_.matmul(p_b1[:, at:at + EXPERTS], bT[:, k, t * P:(t + 1) * P],
                                            gate_sb[:, k, :], start=k == 0, stop=k == KC - 1)
                    ins.then_inc(logits_psum, 1)
                    for n in range(2 * HCH):
                        if n >= 3:
                            wait(pe, up_taken, 2 * HCH * (c - 1) + n - 2)
                        lo = (n % 2) * HALF + (n // 2) * P
                        for k in range(KC):
                            ins = t_.matmul(shared_bank[n % 3][:], sgup_sb[:, k, lo:lo + P], bT[:, k, :],
                                            start=k == 0, stop=k == KC - 1)
                        ins.then_inc(up_psum, 1)
                        if n == 2:
                            ranks(c)

            def ranks(c):
                wait(pe, chosen_ready, c)
                for t in range(TPB + 1):
                    o = p_b1[:, RANKS + t * EXPERTS:RANKS + (t + 1) * EXPERTS]
                    for s in range(t):
                        ins = t_.matmul(o, ones_bf[:], chosen[:, s, :], start=s == 0, stop=s == TPB - 1)
                    if t < TPB:
                        t_.matmul(o, before_bf[:], chosen[:, t, :], start=t == 0, stop=True)
                ins.then_inc(ranks_psum, 1)

            pe.wait_ge(pool_const, 6)
            pe.wait_ge(const_ready, 1)
            pe.wait_ge(weights_in[0], 16 * 7)
            project_x(0, 0, "T")
            project_x(0, 1, "T")
            project_x(0, 0, "P")
            project_x(0, 1, "P")
            pe.wait_ge(weights_in[1], 16 * 3)
            pe.wait_ge(weights_in[2], 16 * 3)
            for c in range(FIRST):
                body(c, True, c >= 1, c >= 2)
            with pe.Fori(FIRST, LAST - 1) as c:
                body(c, True, True, True)
            body(BLOCKS - 1, True, True, True)
            body(BLOCKS, False, True, True)
            body(BLOCKS + 1, False, False, True)

            def expert(k):
                return pe.value_load(tab_ei[0:1, bass.ds(k, 1)], min_val=0, max_val=EXPERTS - 1)

            def exp_w(e, lo, hi):
                return exp_sb[:, bass.ds(e, 1), lo:hi].rearrange("p a n -> p (a n)")

            def gT(k, j):
                pe.wait_ge(xg_loaded[j], 16 * (k // 2 + 1) if isinstance(k, int) else 8 * (k - j) + 16)
                wait(pe, gT_ready, k)
                for c in range(KC):
                    ins = t_.transpose(p_xT[:, c * P:(c + 1) * P], xg[j][:, c * P:(c + 1) * P], ident[:])
                ins.then_inc(gT_psum, 1)

            def gate_up(k, j, e):
                pe.wait_ge(gT_ready, k + 1)
                wait(pe, hg_ready, k - 1)
                for bnk, lo, ready in ((gate_bank[j], 0, gate_psum), (up_bank[j], HALF, gu_psum)):
                    for c in range(KC):
                        at = c * 2 * HALF + lo
                        ins = t_.matmul(bnk[:, 0:HALF], xgT[j][:, c * P:(c + 1) * P],
                                        exp_w(e, at, at + HALF), start=c == 0, stop=c == KC - 1)
                    ins.then_inc(ready, 1)

            def hT(k, j):
                pe.wait_ge(hg_ready, k + 1)
                wait(pe, hgT_ready, k)
                for c in range(HCH):
                    ins = t_.transpose(p_core[:, c * P:(c + 1) * P], hg[:, c * P:(c + 1) * P], ident[:])
                ins.then_inc(hgT_psum, 1)

            def down(k, j, e):
                pe.wait_ge(hgT_ready, k + 1)
                wait(pe, y_ready, k - 1)
                for c in range(HCH):
                    at = KC * 2 * HALF + c * D
                    ins = t_.matmul(y_bank[j][:, 0:D], hgT[j][:, c * P:(c + 1) * P], exp_w(e, at, at + D),
                                    start=c == 0, stop=c == HCH - 1)
                ins.then_inc(y_psum, 1)

            pe.wait_ge(tables_ready, 1)
            pe.wait_ge(experts_in, 16 * EXPERTS)
            gT(0, 0)
            gate_up(0, 0, expert(0))
            gT(1, 1)
            hT(0, 0)
            gate_up(1, 1, expert(1))

            def step(k, j):
                gT(k + 1, 1 - j)
                down(k - 1, 1 - j, expert(k - 1))
                e = expert(k + 1)
                hT(k, j)
                gate_up(k + 1, 1 - j, e)
            step(1, 1)
            step(2, 0)
            with pe.Fori(1, (SORTED_TILES - 2) // 2) as m:
                step(2 * m + 1, 1)
                step(2 * m + 2, 0)
            k = SORTED_TILES - 1
            down(k - 1, 0, expert(k - 1))
            hT(k, 1)
            down(k, 1, expert(k))


def kernel(**inputs):
    import numpy as np
    import concourse.bacc as bacc
    from concourse.bass_utils import run_bass_kernel_spmd

    def get(name):
        return np.asarray(inputs["L0_" + name])

    def rows_of(w):
        return w.reshape(-1, P, w.shape[-1]).transpose(1, 0, 2)

    w_up, w_down = get("ffn_w_up"), get("ffn_w_down")
    experts = np.concatenate([
        w_up.transpose(0, 2, 1).reshape(EXPERTS, KC, P, 2 * HALF).transpose(0, 2, 1, 3).reshape(EXPERTS, P, -1),
        w_down.transpose(0, 2, 1).reshape(EXPERTS, HCH, P, D).transpose(0, 2, 1, 3).reshape(EXPERTS, P, -1),
    ], axis=2)
    arrays = {
        "x": get("attn_q_x").reshape(TOKENS, D),
        "wqkv": rows_of(np.concatenate([get("attn_wq"), get("attn_wk"), get("attn_wv")], axis=1)),
        "b_tok": np.concatenate([get(f"attn_{n}") for n in ("bq", "bk", "bv", "bo", "proj_b")])[None],
        "ln1w": get("attn_ln1_w").reshape(KC, P).T,
        "ln1b": get("attn_ln1_b").reshape(KC, P).T,
        "ln2w": get("attn_ln2_w").reshape(KC, P).T,
        "ln2b": get("attn_ln2_b").reshape(KC, P).T,
        "wo": rows_of(get("attn_wo")),
        "fc_w": rows_of(get("attn_fc_w")),
        "fc_b": get("attn_fc_b").reshape(FCH, P).T,
        "proj_w": rows_of(get("attn_proj_w")),
        "gate_w": rows_of(get("ffn_gate_w").T),
        "sg_up": rows_of(np.concatenate([get("ffn_sg_gate"), get("ffn_sg_up")], axis=0).T),
        "sg_down": rows_of(get("ffn_sg_down").T),
        "experts": experts,
    }
    nc = bacc.Bacc("TRN2", target_bir_lowering=False, num_devices=1)
    feeds, args = {}, []
    for name, a in arrays.items():
        feeds[f"in_{name}"] = np.ascontiguousarray(a)
        args.append(nc.dram_tensor(f"in_{name}", list(a.shape), mybir.dt.from_np(a.dtype),
                                   kind="ExternalInput").ap())
    args.append(nc.dram_tensor("out_rows", [TOKENS + P, D], FP32, kind="ExternalOutput").ap())
    build(nc, *args)
    result = run_bass_kernel_spmd(nc, [feeds], core_ids=[0]).results[0]
    return result["out_rows"][0:TOKENS].reshape(16, 512, D)
```

```python
from contextlib import ExitStack

import concourse.bass as bass
from concourse import mybir

FP32 = mybir.dt.float32
BF16 = mybir.dt.bfloat16
INT32 = mybir.dt.int32
UINT32 = mybir.dt.uint32
ALU = mybir.AluOpType
ACT = mybir.ActivationFunctionType
AX = mybir.AxisListType

P = 128
TOKENS = 16 * 512
D = 256
KC = D // P
HEADS = 16
HD = D // HEADS
MLP = 4 * D
FCH = MLP // P
EXPERTS = 8
HALF = 384
HCH = HALF // P
TPB = 4
BLOCK = TPB * P
BLOCKS = TOKENS // BLOCK
EPS = 1e-5

REGION = TOKENS + P
SORTED_TILES = 2 * TOKENS // P + EXPERTS - 1
SPARE_TILES = EXPERTS
ROW = D + 4
C_TOK, C_W0, C_W1, C_E0 = D, D + 1, D + 2, D + 3
EXW = KC * 2 * HALF + HCH * D

POOL_TILE = 3
DVE_HEADS = 12
POOL_HEADS = HEADS - DVE_HEADS
ORDER = (POOL_TILE, 0, 1, 2)
POOL_STEPS, DVE_STEPS = 23, 82
HE = HD + 1


def build(nc, x, wqkv, b_tok, ln1w, ln1b, ln2w, ln2b, wo, fc_w, fc_b, proj_w, gate_w, sg_up, sg_down,
          experts, out):
    ctx = ExitStack()
    with ctx:
        def sb(name, shape, dt=FP32):
            return ctx.enter_context(nc.sbuf_tensor(name, shape, dt))

        def sem(name):
            return ctx.enter_context(nc.semaphore(name))

        x_blk = x.rearrange("(b t p) d -> b p t d", t=TPB, p=P)
        out_blk = out[0:TOKENS, :].rearrange("(b t p) d -> b p t d", t=TPB, p=P)
        rows_sorted = nc.dram_tensor("rows_sorted", [EXPERTS * REGION + SPARE_TILES * P, ROW], FP32,
                                     kind="Internal").ap()

        wqkv_sb = sb("wqkv_sb", [P, KC, 3 * D])
        wo_sb = sb("wo_sb", [P, KC, D])
        fc_sb = sb("fc_sb", [P, KC, MLP])
        proj_sb = sb("proj_sb", [P, FCH, D])
        gate_sb = sb("gate_sb", [P, KC, EXPERTS])
        sgup_sb = sb("sgup_sb", [P, KC, 2 * HALF])
        sgdn_sb = sb("sgdn_sb", [P, HCH, D])
        exp_sb = sb("exp_sb", [P, EXPERTS, EXW])
        ln_sb = sb("ln_sb", [P, 4, KC])
        fcb_sb = sb("fcb_sb", [P, FCH])
        ones_bf = sb("ones_bf", [P, P], BF16)
        before_bf = sb("before_bf", [P, P], BF16)
        bias_bf = sb("bias_bf", [P, 5 * D], BF16)
        ident = sb("ident", [P, P])

        xin = sb("xin", [P, TPB, D])
        xnT = [sb(f"xnT{j}", [P, KC, P]) for j in range(2)]
        eqk = sb("eqk", [P, 2 * D])
        rqk = sb("rqk", [P, 2 * D])
        v_dve = [sb(f"v_dve{j}", [P, HD, HEADS]) for j in range(2)]
        v_pool = sb("v_pool", [P, HEADS, HE])
        fq = [sb(f"fq{j}", [P, HEADS, HD]) for j in range(2)]
        fqk_pool = sb("fqk_pool", [P, 2, HEADS, HD])
        prod = sb("prod", [P, HEADS * HE * HD])
        prod_pool = sb("prod_pool", [P, HEADS * HE * HD])
        qkv = [sb(f"qkv{j}", [P, HEADS, HE]) for j in range(2)]
        kvT_pool = sb("kvT_pool", [P, HE, HD])
        kv_pool = sb("kv_pool", [P, HD, HE])
        qkv_pool = sb("qkv_pool", [P, HEADS, HE])
        attn = sb("attn", [P, TPB, D])
        xres = sb("xres", [P, TPB, D])
        xmid = sb("xmid", [P, TPB, D])
        bT = sb("bT", [P, KC, BLOCK])
        hid = sb("hid", [P, FCH, BLOCK])
        x1 = sb("x1", [P, TPB, D])
        rows = sb("rows", [P, TPB, ROW])
        sg_g = hid[:, 0:HCH, :]
        sg_u = hid[:, HCH:2 * HCH, :]
        hnorm = hid[:, FCH - 2:FCH, :].rearrange("p a (t d) -> p (a t) d", d=D)
        st6 = sb("st6", [P, TPB, 6])
        mv_a = sb("mv_a", [P, TPB, 2])
        sq_a = sb("sq_a", [P, 2, TPB])
        rs_a = sb("rs_a", [P, 3, TPB])
        a_scale = sb("a_scale", [P, 2, TPB])
        mv_b = sb("mv_b", [P, TPB, 2])
        sq_b = sb("sq_b", [P, TPB])
        rs_b = sb("rs_b", [P, 2, TPB])
        den = sb("den", [P, 2, HEADS])
        act_tmp = sb("act_tmp", [P, 4])
        top_v = sb("top_v", [P, TPB, 8])
        top_i = sb("top_i", [P, TPB, 8], UINT32)
        iota_e = sb("iota_e", [P, EXPERTS])
        iota_r = sb("iota_r", [P, EXPERTS])
        first2 = sb("first2", [P, 2, TPB])
        gap = sb("gap", [P, TPB])
        gap_e = sb("gap_e", [P, TPB])
        onehot = sb("onehot", [P, 2, TPB, EXPERTS])
        chosen = sb("chosen", [P, TPB, EXPERTS], BF16)
        free_row = sb("free_row", [P, EXPERTS])
        rank = sb("rank", [P, TPB, EXPERTS])
        slot_w = sb("slot_w", [P, 2, TPB, EXPERTS])
        slot = sb("slot", [P, 2 * TPB], INT32)
        tok = sb("tok", [P, TPB])
        pad_row = sb("pad_row", [P, ROW])
        pad_at = sb("pad_at", [P, EXPERTS], INT32)
        iota_p = sb("iota_p", [P, 1])
        def carver(buffer):
            used = [0]

            def piece(n):
                used[0] += n
                assert used[0] <= buffer.shape[1]
                return buffer[:, used[0] - n:used[0]]
            return piece
        piece, piece_pool = carver(prod), carver(prod_pool)
        xg = [piece(ROW) for _ in range(2)]
        xgT = [piece(D) for _ in range(2)]
        hg = piece(HALF)
        hact = piece(HALF)
        hgT = [piece(HALF) for _ in range(2)]
        tab_e = piece(SORTED_TILES)
        tab_ei = piece(SORTED_TILES).bitcast(INT32)
        tab_row = piece(SORTED_TILES).bitcast(INT32)
        tiles_f = piece(EXPERTS)
        tiles_to = piece(EXPERTS)
        cnt_i = piece(EXPERTS).bitcast(INT32)
        w_row = [piece(1) for _ in range(2)]
        tok_i = [piece(1).bitcast(INT32) for _ in range(2)]
        w_tmp = piece(2)
        meta = piece(ROW - D)
        yg = [piece_pool(D) for _ in range(2)]
        tab_first = piece_pool(SORTED_TILES)
        iota_k = piece_pool(SORTED_TILES)
        bias_hi = prod_pool[:, 0:5 * D // 2].bitcast(BF16)

        def bank(name):
            return ctx.enter_context(nc.psum_tensor(name, [P, 512], FP32))
        p_xT, p_q0, p_q1, p_core, p_b0, p_b1, p_b2, p_b3 = (
            bank(n) for n in ("p_xT", "p_q0", "p_q1", "p_core", "p_b0", "p_b1", "p_b2", "p_b3"))
        shared_bank = (p_b0, p_b2, p_b3)
        LOGITS, RANKS = 0, 2 * TPB * EXPERTS
        gate_bank, up_bank, y_bank = (p_q0, p_b0), (p_q1, p_b1), (p_b2, p_b3)

        weights_in = [sem(f"weights_in{j}") for j in range(3)]
        experts_in = sem("experts_in")
        pool_const = sem("pool_const")
        const_ready = sem("const_ready")
        tmp_ready = sem("tmp_ready")
        bias_ready = sem("bias_ready")
        xin_loaded = sem("xin_loaded")
        ln1_var = sem("ln1_var")
        ln1_std = sem("ln1_std")
        ln1_scale = sem("ln1_scale")
        xhat_ready = sem("xhat_ready")
        scale_ready = sem("scale_ready")
        xT_psum = sem("xT_psum")
        xnT_ready = sem("xnT_ready")
        qkv_psum = sem("qkv_psum")
        qkv_taken = sem("qkv_taken")
        feat_ready = sem("feat_ready")
        pool_v_used = sem("pool_v_used")
        pool_qkv = sem("pool_qkv")
        share_ready = sem("share_ready")
        share_done = sem("share_done")
        attn_ready = sem("attn_ready")
        attnT_psum = sem("attnT_psum")
        attnT_ready = sem("attnT_ready")
        xres_loaded = sem("xres_loaded")
        a_ready = sem("a_ready")
        wo_psum = sem("wo_psum")
        ln2_var = sem("ln2_var")
        ln2_std = sem("ln2_std")
        ln2_scale = sem("ln2_scale")
        xsum_ready = sem("xsum_ready")
        h_ready = sem("h_ready")
        hT_psum = sem("hT_psum")
        hT_ready = sem("hT_ready")
        fc_psum = sem("fc_psum")
        gelu_ready = sem("gelu_ready")
        proj_psum = sem("proj_psum")
        x1_read = sem("x1_read")
        ln3_std = sem("ln3_std")
        ln3_scale = sem("ln3_scale")
        rows_ready = sem("rows_ready")
        x3T_psum = sem("x3T_psum")
        x3T_ready = sem("x3T_ready")
        logits_psum = sem("logits_psum")
        gap_ready = sem("gap_ready")
        gap_exp = sem("gap_exp")
        chosen_ready = sem("chosen_ready")
        ranks_psum = sem("ranks_psum")
        ranks_read = sem("ranks_read")
        slots_ready = sem("slots_ready")
        scattered = sem("scattered")
        up_psum = sem("up_psum")
        up_taken = sem("up_taken")
        shared_h = sem("shared_h")
        down_psum = sem("down_psum")
        out_ready = sem("out_ready")
        out_stored = sem("out_stored")
        dve_done = sem("dve_done")
        pool_done = sem("pool_done")
        init_stored = sem("init_stored")
        pads_at = sem("pads_at")
        pads_stored = sem("pads_stored")
        waits_passed = sem("waits_passed")
        tables_ready = sem("tables_ready")
        xg_loaded = [sem(f"xg_loaded{j}") for j in range(2)]
        xg_meta = sem("xg_meta")
        w_ready = sem("w_ready")
        gT_psum = sem("gT_psum")
        gT_ready = sem("gT_ready")
        gate_psum = sem("gate_psum")
        gu_psum = sem("gu_psum")
        g_act = sem("g_act")
        hg_ready = sem("hg_ready")
        hgT_psum = sem("hgT_psum")
        hgT_ready = sem("hgT_ready")
        y_psum = sem("y_psum")
        y_ready = sem("y_ready")
        added = sem("added")

        def wait(eng, s, value):
            if not isinstance(value, int) or value > 0:
                eng.wait_ge(s, value)

        def stand_alone(eng):
            eng.sem_inc(waits_passed, 1)

        class Chain:

            def __init__(self, eng, s):
                self.eng, self.s, self.base, self.n = eng, s, 0, 0

            def __call__(self, ins):
                self.later(ins)
                self.sync()

            def later(self, ins):
                self.n += 1
                ins.then_inc(self.s, 1)
                return self.n

            def reached(self, n):
                self.eng.wait_ge(self.s, self.base + n)

            def sync(self):
                self.eng.wait_ge(self.s, self.base + self.n)

            def enter(self, done, per_round):
                self.before, self.per_round = self.base + self.n, per_round
                self.base, self.n = self.before + done * per_round, 0

            def leave(self, rounds):
                assert self.n == self.per_round, f"{self.n} steps in a round"
                self.base, self.n = self.before + rounds * self.per_round, 0

        def announce(eng, ins, s, value):
            ins.then_inc(s, 1)
            eng.wait_ge(s, value)

        FIRST, LAST = 3, BLOCKS

        block = ctx.enter_context(nc.Block())

        @block.sync
        def _(sp):
            sp.dma_start(xin[:], x_blk[0]).then_inc(xin_loaded, 16)
            for dst, src in ((wqkv_sb, wqkv), (ln_sb[:, 0, :], ln1w), (ln_sb[:, 1, :], ln1b),
                             (ln_sb[:, 2, :], ln2w), (ln_sb[:, 3, :], ln2b), (fcb_sb, fc_b)):
                sp.dma_start(dst[:] if dst in (wqkv_sb, fcb_sb) else dst, src).then_inc(weights_in[0], 16)
            sp.dma_start(prod[:, 0:5 * D], b_tok.to_broadcast([P, 5 * D])).then_inc(weights_in[0], 16)
            for dst, src in ((wo_sb, wo), (fc_sb, fc_w), (proj_sb, proj_w)):
                sp.dma_start(dst[:], src).then_inc(weights_in[1], 16)
            for dst, src in ((gate_sb, gate_w), (sgup_sb, sg_up), (sgdn_sb, sg_down)):
                sp.dma_start(dst[:], src).then_inc(weights_in[2], 16)

            sp.wait_ge(const_ready, 1)
            sp.dma_start(rows_sorted[EXPERTS * REGION:, :].rearrange("(j p) d -> p j d", p=P),
                         pad_row[:].unsqueeze(1).to_broadcast([P, SPARE_TILES, ROW])
                         ).then_inc(init_stored, 16)
            sp.dma_start(out[TOKENS:TOKENS + P, :], pad_row[:, 0:D]).then_inc(init_stored, 16)

            def body(c, core, stage_b, tail):
                if stage_b:
                    wait(sp, x1_read, c - 1)
                    sp.dma_start(xres[:], x_blk[bass.ds(c - 1, 1)].rearrange("b p t d -> p (b t) d")
                                 ).then_inc(xres_loaded, 16)
                if core and (not isinstance(c, int) or c < BLOCKS - 1):
                    wait(sp, xT_psum, 4 * (c + 1))
                    sp.dma_start(xin[:], x_blk[bass.ds(c + 1, 1)].rearrange("b p t d -> p (b t) d")
                                 ).then_inc(xin_loaded, 16)
                if isinstance(c, int) and c in (1, 2):
                    for e in range((c - 1) * EXPERTS // 2, c * EXPERTS // 2):
                        sp.dma_start(exp_sb[:, e, :], experts[e]).then_inc(experts_in, 16)
                if tail:
                    wait(sp, out_ready, c - 1)
                    sp.dma_start(out_blk[bass.ds(c - 2, 1)].rearrange("b p t d -> p (b t) d"), x1[:]
                                 ).then_inc(out_stored, 16)

            for c in range(FIRST):
                body(c, True, c >= 1, c >= 2)
            with sp.Fori(FIRST, LAST - 1) as c:
                body(c, True, True, True)
            body(BLOCKS - 1, True, True, True)
            body(BLOCKS, False, True, True)

            sp.wait_ge(pads_at, 1)
            for e in range(EXPERTS):
                row = sp.value_load(pad_at[0:1, e:e + 1], min_val=0, max_val=EXPERTS * REGION - P)
                sp.dma_start(rows_sorted[bass.ds(row, P), :], pad_row[:]).then_inc(pads_stored, 16)

            sp.wait_ge(tables_ready, 1)
            sp.wait_ge(init_stored, 32)
            sp.wait_ge(pads_stored, 16 * EXPERTS)
            sp.wait_ge(scattered, 16 * 2 * TPB * BLOCKS)

            def load(k, j):
                row = sp.value_load(tab_row[0:1, bass.ds(k, 1)], min_val=0,
                                    max_val=EXPERTS * REGION + (SPARE_TILES - 1) * P)
                wait(sp, gT_psum, k - 1)
                wait(sp, xg_meta, k - 1)
                sp.dma_start(xg[j], rows_sorted[bass.ds(row, P), :]).then_inc(xg_loaded[j], 16)
            load(0, 0)
            load(1, 1)
            body(BLOCKS + 1, False, False, True)
            with sp.Fori(1, SORTED_TILES // 2) as m:
                load(2 * m, 0)
                load(2 * m + 1, 1)
            load(SORTED_TILES - 1, 0)
            sp.wait_ge(out_stored, 16 * BLOCKS)
            sp.wait_ge(added, 16 * SORTED_TILES)

        @block.gpsimd
        def _(pool):
            g = nc.gpsimd
            done = Chain(pool, pool_done)
            done(g.memset(ident[:], 0.0))
            g.affine_select(out=ident[:], in_=ident[:], compare_op=ALU.not_equal, fill=1.0, base=0,
                            pattern=[[-1, P]], channel_multiplier=1).then_inc(pool_const, 1)
            done(g.memset(ones_bf[:], 1.0))
            g.affine_select(out=before_bf[:], in_=ones_bf[:], compare_op=ALU.is_gt, fill=0.0, base=0,
                            pattern=[[1, P]], channel_multiplier=-1).then_inc(pool_const, 1)
            done(g.memset(v_pool[:], 1.0))
            g.iota(iota_e[:], [[1, EXPERTS]], base=0, channel_multiplier=0,
                   allow_small_or_imprecise_dtypes=True).then_inc(pool_const, 1)
            g.iota(iota_r[:], [[REGION, EXPERTS]], base=0, channel_multiplier=0,
                   allow_small_or_imprecise_dtypes=True).then_inc(pool_const, 1)
            g.iota(tok[:], [[P, TPB]], base=-BLOCK, channel_multiplier=1,
                   allow_small_or_imprecise_dtypes=True).then_inc(pool_const, 1)
            g.iota(iota_p[:], [[0, 1]], base=0, channel_multiplier=1,
                   allow_small_or_imprecise_dtypes=True).then_inc(pool_const, 1)

            def halve_once(at, w, n):
                done(g.tensor_tensor(prod_pool[:, at:at + n * w], prod_pool[:, at:at + n * w],
                                     prod_pool[:, at + n * w:at + 2 * n * w], ALU.add))

            def halve(dst, at=0, first=8):
                w = dst.shape[-1]
                n = first
                while n > 1:
                    halve_once(at, w, n)
                    n //= 2
                return g.tensor_tensor(dst, prod_pool[:, at:at + w], prod_pool[:, at + w:at + 2 * w], ALU.add)

            def heads(c, u):
                wait(pool, share_ready, 3 * c + u)
                n = HD * POOL_HEADS * HE
                at = HEADS * HE * HD // 2
                done(g.tensor_tensor(
                    prod_pool[:, at:at + n].rearrange("p (d h e) -> p d h e", d=HD, e=HE),
                    fq[u % 2][:, DVE_HEADS:, :].rearrange("p h d -> p d h").unsqueeze(3)
                    .to_broadcast([P, HD, POOL_HEADS, HE]),
                    kvT_pool[:].rearrange("p e d -> p d e").unsqueeze(2)
                    .to_broadcast([P, HD, POOL_HEADS, HE]), ALU.mult))
                announce(pool, halve(qkv[u % 2][:, DVE_HEADS:, :].rearrange("p h e -> p (h e)"), at),
                         share_done, 3 * c + u)

            def scatter(c):
                wait(pool, slots_ready, c - 1)
                stand_alone(pool)
                done.later(g.tensor_scalar(tok[:], tok[:], float(BLOCK), None, ALU.add))
                done(g.tensor_copy(rows[:, :, C_E0], first2[:, 0, :]))
                stand_alone(pool)
                done(g.tensor_copy(rows[:, :, C_TOK], tok[:]))
                stand_alone(pool)
                for s in range(2):
                    for t in range(TPB):
                        pool.indirect_dma_start(
                            out=rows_sorted[:, :],
                            out_offset=bass.IndirectOffsetOnAxis(
                                ap=slot[:, s * TPB + t:s * TPB + t + 1], axis=0),
                            in_=rows[:, t, :], in_offset=None).then_inc(scattered, 16)

            def gate_shared(c):
                wait(pool, up_taken, 2 * HCH * (c - 1))
                announce(pool, g.tensor_tensor(sg_g, sg_g, sg_u, ALU.mult), shared_h, c - 1)

            def body(c, core, stage_b, tail):
                if tail and (core or stage_b):
                    gate_shared(c)
                if core:
                    wait(pool, feat_ready, 4 * c + 1)
                    done(g.tensor_tensor(
                        prod_pool[:].rearrange("p (h d e) -> p h d e", h=HEADS, d=HD),
                        fqk_pool[:, 1].unsqueeze(3).to_broadcast([P, HEADS, HD, HE]),
                        v_pool[:].unsqueeze(2).to_broadcast([P, HEADS, HD, HE]), ALU.mult))
                    halve_once(0, HD * HE, 8)
                    heads(c, 1)
                    announce(pool, halve(kv_pool[:].rearrange("p d e -> p (d e)"), first=4), pool_v_used, c + 1)
                if tail:
                    scatter(c)
                if stage_b:
                    wait(pool, xres_loaded, 16 * c)
                    wait(pool, ln2_var, c)
                    announce(pool, g.tensor_tensor(xres[:], xres[:], xmid[:], ALU.add), xsum_ready, c)
                if core:
                    heads(c, 2)
                    done(g.tensor_tensor(
                        prod_pool[:].rearrange("p (d h e) -> p d h e", d=HD, h=HEADS),
                        fqk_pool[:, 0].rearrange("p h d -> p d h").unsqueeze(3)
                        .to_broadcast([P, HD, HEADS, HE]),
                        kv_pool[:].unsqueeze(2).to_broadcast([P, HD, HEADS, HE]), ALU.mult))
                    announce(pool, halve(qkv_pool[:].rearrange("p h e -> p (h e)")), pool_qkv, c + 1)
                    heads(c, 3)

            for c in range(FIRST):
                body(c, True, c >= 1, c >= 2)
            with pool.Fori(FIRST, LAST) as c:
                done.enter(c - FIRST, POOL_STEPS)
                body(c, True, True, True)
                done.leave(LAST - FIRST)
            body(BLOCKS, False, True, True)
            g.iota(iota_k, [[1, SORTED_TILES]], base=0, channel_multiplier=0,
                   allow_small_or_imprecise_dtypes=True).then_inc(pool_const, 1)
            body(BLOCKS + 1, False, False, True)

            pool.wait_ge(out_stored, 16 * BLOCKS)
            pool.wait_ge(init_stored, 32)

            def add(k, j):
                pool.wait_ge(y_ready, k + 1)
                wait(pool, added, 16 * k)
                stand_alone(pool)
                pool.indirect_dma_start(out=out[:, :],
                                        out_offset=bass.IndirectOffsetOnAxis(ap=tok_i[j], axis=0),
                                        in_=yg[j], in_offset=None, compute_op=ALU.add).then_inc(added, 16)
            add(0, 0)
            add(1, 1)
            with pool.Fori(1, SORTED_TILES // 2) as m:
                add(2 * m, 0)
                add(2 * m + 1, 1)
            add(SORTED_TILES - 1, 0)

        @block.scalar
        def _(act):
            a = nc.scalar

            def take_x(c, u):
                n = 4 * c + u
                wait(act, xT_psum, n + 1)
                wait(act, qkv_psum, n - 1)
                for k in range(KC):
                    ins = a.activation(xnT[u % 2][:, k, :], p_xT[:, k * P:(k + 1) * P], ACT.Identity,
                                       bias=ln_sb[:, 1, k:k + 1], scale=ln_sb[:, 0, k:k + 1])
                ins.then_inc(xnT_ready, 1)

            def take_qkv(c, u):
                n = 4 * c + u
                wait(act, qkv_psum, n + 1)
                wait(act, feat_ready, n)
                a.activation(eqk[:], p_q0[:], ACT.Exp)
                a.activation(rqk[:], p_q0[:], ACT.Relu)
                v = p_q1[:, 0:D].rearrange("p (h e) -> p h e", h=HEADS)
                if u == 0:
                    wait(act, pool_v_used, c)
                    ins = a.activation(v_pool[:, :, 0:HD], v, ACT.Copy)
                else:
                    ins = a.activation(v_dve[u % 2][:].rearrange("p e h -> p h e"), v, ACT.Copy)
                ins.then_inc(qkv_taken, 1)

            def norm(dst, src, scales, ready):
                for t in range(TPB):
                    a.activation(dst(t), src(t), ACT.Identity, bias=scales[:, 1, t:t + 1],
                                 scale=scales[:, 0, t:t + 1]).then_inc(ready, 1)

            def norm_1(b):
                wait(act, ln1_scale, b + 1)
                norm(lambda t: xin[:, t, :], lambda t: xin[:, t, :], rs_a[:, 1:3], xhat_ready)

            def take_pair(c, banks, psum, ready):
                for k, bnk in enumerate(banks):
                    wait(act, psum, KC * (c - 1) + k + 1)
                    a.activation(bT[:, k, :], bnk[:], ACT.Copy).then_inc(ready, 1)

            def take_shared(c, parts):
                for n in parts:
                    wait(act, up_psum, 2 * HCH * (c - 1) + n + 1)
                    dst, func = ((sg_g, ACT.Silu), (sg_u, ACT.Copy))[n % 2]
                    a.activation(dst[:, n // 2, :], shared_bank[n % 3][:], func).then_inc(up_taken, 1)

            def table(func, at=1):
                a.activation(act_tmp[:, at:at + 1], act_tmp[:, 0:1], func)

            def body(c, core, stage_b, tail):
                more = core and (not isinstance(c, int) or c < BLOCKS - 1)
                if core:
                    take_x(c, 2)
                if stage_b:
                    take_pair(c, (p_b0, p_b1), attnT_psum, attnT_ready)
                if core:
                    take_x(c, 3)
                if stage_b:
                    wait(act, xres_loaded, 16 * c)
                    wait(act, scale_ready, c)
                    wait(act, xsum_ready, c - 1)
                    norm(lambda t: xmid[:, t, :], lambda t: xres[:, t, :], a_scale, a_ready)
                if core:
                    table(ACT.Exp, 3)
                    take_qkv(c, 2)
                if stage_b:
                    table(ACT.Sqrt)
                    wait(act, ln2_var, c)
                    a.activation(sq_b[:], sq_b[:], ACT.Sqrt).then_inc(ln2_std, 1)
                    wait(act, ln2_scale, c)
                    wait(act, proj_psum, 2 * (c - 1))
                    norm(lambda t: hnorm[:, t, :], lambda t: xmid[:, t, :], rs_b, h_ready)
                if more:
                    wait(act, ln1_var, c + 2)
                    a.activation(sq_a[:], sq_a[:], ACT.Sqrt).then_inc(ln1_std, 1)
                if stage_b:
                    for k, bnk in enumerate((p_b2, p_b3)):
                        wait(act, hT_psum, KC * (c - 1) + k + 1)
                        a.activation(bT[:, k, :], bnk[:], ACT.Identity, bias=ln_sb[:, 3, k:k + 1],
                                     scale=ln_sb[:, 2, k:k + 1]).then_inc(hT_ready, 1)
                    table(ACT.Gelu)
                    for f in range(FCH):
                        wait(act, fc_psum, FCH * (c - 1) + f + 1)
                        if f == 0:
                            wait(act, down_psum, c - 2)
                        a.activation(hid[:, f, :], (p_b2, p_b3)[f % 2][:], ACT.Gelu,
                                     bias=fcb_sb[:, f:f + 1]).then_inc(gelu_ready, 1)
                if core:
                    take_qkv(c, 3)
                if more:
                    norm_1(c + 1)
                    take_x(c + 1, 0)
                    take_x(c + 1, 1)
                    take_qkv(c + 1, 0)
                if stage_b:
                    table(ACT.Sqrt)
                    wait(act, x1_read, c)
                    a.activation(sq_b[:], sq_b[:], ACT.Sqrt).then_inc(ln3_std, 1)
                    wait(act, ln3_scale, c)
                    wait(act, scattered, 16 * 2 * TPB * (c - 1))
                    norm(lambda t: rows[:, t, 0:D], lambda t: x1[:, t, :], rs_b, rows_ready)
                    take_pair(c, (p_b2, p_b3), x3T_psum, x3T_ready)
                    table(ACT.Silu)
                    take_shared(c, range(3))
                if more:
                    take_qkv(c + 1, 1)
                if stage_b:
                    wait(act, gap_ready, c)
                    a.activation(gap_e[:], gap[:], ACT.Exp).then_inc(gap_exp, 1)
                    table(ACT.Silu, 2)
                    take_shared(c, range(3, 2 * HCH))

            act.wait_ge(pool_const, 3)
            act.wait_ge(tmp_ready, 1)
            wait(act, ln1_var, 1)
            a.activation(sq_a[:], sq_a[:], ACT.Sqrt).then_inc(ln1_std, 1)
            norm_1(0)
            act.wait_ge(weights_in[0], 16 * 7)
            take_x(0, 0)
            take_x(0, 1)
            take_qkv(0, 0)
            take_qkv(0, 1)
            for c in range(FIRST):
                body(c, True, c >= 1, c >= 2)
            with act.Fori(FIRST, LAST - 1) as c:
                body(c, True, True, True)
            body(BLOCKS - 1, True, True, True)
            body(BLOCKS, False, True, True)

            def take_gT(k, j):
                act.wait_ge(gT_psum, k + 1)
                wait(act, gu_psum, k - 1)
                a.activation(xgT[j], p_xT[:, 0:D], ACT.Copy).then_inc(gT_ready, 1)

            def silu(k, j):
                act.wait_ge(gate_psum, k + 1)
                wait(act, hg_ready, k)
                a.activation(hact, gate_bank[j][:, 0:HALF], ACT.Silu).then_inc(g_act, 1)

            def weigh(k, j):
                act.wait_ge(y_psum, k + 1)
                wait(act, w_ready, k + 1)
                wait(act, added, 16 * (k - 1))
                a.activation(yg[j], y_bank[j][:, 0:D], ACT.Copy, scale=w_row[j]).then_inc(y_ready, 1)

            act.wait_ge(tables_ready, 1)
            take_gT(0, 0)
            silu(0, 0)
            take_gT(1, 1)

            def pair(k, j):
                silu(k, j)
                take_gT(k + 1, 1 - j)
                weigh(k - 1, 1 - j)
            pair(1, 1)
            pair(2, 0)
            with act.Fori(1, (SORTED_TILES - 3) // 2) as m:
                pair(2 * m + 1, 1)
                pair(2 * m + 2, 0)
            pair(SORTED_TILES - 2, 1)
            silu(SORTED_TILES - 1, 0)
            weigh(SORTED_TILES - 2, 1)
            weigh(SORTED_TILES - 1, 0)

        @block.vector
        def _(dve):
            v = nc.vector
            done = Chain(dve, dve_done)

            def stats(src, mv):
                for t in range(TPB):
                    done.later(v.bn_stats(st6[:, t, :], src(t)))
                averages(mv)

            def averages(mv):
                done.sync()
                stand_alone(dve)
                for t in range(TPB):
                    done.later(v.bn_aggr(mv[:, t, :], st6[:, t, :]))
                done.sync()

            def ln1_stats(b):
                wait(dve, xin_loaded, 16 * (b + 1))
                stats(lambda t: xin[:, t, :], mv_a)
                done.later(v.tensor_scalar(sq_a[:, 0, :], mv_a[:, :, 1], 1.0, EPS, ALU.mult, ALU.add))
                v.tensor_scalar(sq_a[:, 1, :], mv_a[:, :, 1], 1.0 + EPS, EPS * EPS,
                                              ALU.mult, ALU.add).then_inc(ln1_var, 1)

            def ln1_scales(b):
                wait(dve, ln1_std, b + 1)
                done(v.reciprocal(rs_a[:, 0:2], sq_a[:]))
                v.scalar_tensor_tensor(rs_a[:, 2, :], mv_a[:, :, 0], -1.0, rs_a[:, 1, :],
                                                     ALU.mult, ALU.mult).then_inc(ln1_scale, 1)

            def scales_b(std, scale, c):
                wait(dve, std, c)
                done(v.reciprocal(rs_b[:, 0], sq_b[:]))
                v.scalar_tensor_tensor(rs_b[:, 1, :], mv_b[:, :, 0], -1.0, rs_b[:, 0, :],
                                                     ALU.mult, ALU.mult).then_inc(scale, 1)

            def keep_scales(c):
                wait(dve, a_ready, TPB * c)
                done.later(v.tensor_copy(a_scale[:, 0, :], rs_a[:, 0, :]))
                v.scalar_tensor_tensor(a_scale[:, 1, :], mv_a[:, :, 0], -1.0, rs_a[:, 0, :],
                                                     ALU.mult, ALU.mult).then_inc(scale_ready, 1)

            def features(c, u):
                n = 4 * c + u
                wait(dve, qkv_taken, n + 1)
                if u == 0:
                    ins = v.scalar_tensor_tensor(fqk_pool[:].rearrange("p a h d -> p (a h d)"), eqk[:], 1.0,
                                                 rqk[:], ALU.min, ALU.add)
                else:
                    done.later(v.scalar_tensor_tensor(fq[u % 2][:].rearrange("p h d -> p (h d)"), eqk[:, 0:D], 1.0,
                                                      rqk[:, 0:D], ALU.min, ALU.add))
                    ins = v.scalar_tensor_tensor(
                        fkT, eqk[:, D:2 * D].rearrange("p (h d) -> p d h", h=HEADS), 1.0,
                        rqk[:, D:2 * D].rearrange("p (h d) -> p d h", h=HEADS), ALU.min, ALU.add)
                ins.then_inc(feat_ready, 1)
                if u > 0:
                    dve.wait_ge(feat_ready, n + 1)

            fkT = p_core[:, 0:D].rearrange("p (d h) -> p d h", d=HD)
            kv_first = 512 - HE * HD
            kvT = p_core[:, kv_first:512].rearrange("p (e d) -> p e d", e=HE)

            def kv_products(u):
                done.later(v.tensor_reduce(kvT[:, HD, :], fkT, AX.X, ALU.add))
                done.later(v.tensor_tensor(
                    prod[:, 0:HD * HD * HEADS].rearrange("p (e d h) -> p e d h", e=HD, d=HD),
                    fkT.unsqueeze(1).to_broadcast([P, HD, HD, HEADS]),
                    v_dve[u % 2][:].unsqueeze(2).to_broadcast([P, HD, HD, HEADS]), ALU.mult))

            def kv_sums(half):
                n = HD * HD // 2
                done.later(v.tensor_reduce(
                    p_core[:, kv_first + half * n:kv_first + (half + 1) * n],
                    prod[:, half * n * HEADS:(half + 1) * n * HEADS].rearrange("p (a h) -> p a h", h=HEADS),
                    AX.X, ALU.add))

            def share(c, u):
                done.sync()
                v.tensor_copy(kvT_pool[:], kvT).then_inc(share_ready, 1)

            def q_products(u):
                done.sync()
                n = DVE_HEADS
                done.later(v.tensor_tensor(
                    prod[:, 0:n * HE * HD].rearrange("p (h e d) -> p h e d", h=n, e=HE),
                    fq[u % 2][:, 0:n].unsqueeze(2).to_broadcast([P, n, HE, HD]),
                    kvT.unsqueeze(1).to_broadcast([P, n, HE, HD]), ALU.mult))

            def q_sums(u):
                done.sync()
                n = DVE_HEADS
                done.later(v.tensor_reduce(
                    qkv[u % 2][:, 0:n].rearrange("p h e -> p (h e)"),
                    prod[:, 0:n * HE * HD].rearrange("p (a d) -> p a d", d=HD), AX.X, ALU.add))

            def divide_1(src, i=0):
                return done.later(v.tensor_scalar(den[:, i], src[:, :, HD], 1e-6, None, ALU.add))

            def divide_2(first, i=0):
                done.reached(first)
                return done.later(v.reciprocal(den[:, i], den[:, i]))

            def divide_3(second, c, t, src, i=0):
                done.reached(second)
                return v.tensor_tensor(attn[:, t, :].rearrange("p (h e) -> p h e", h=HEADS),
                                       src[:, :, 0:HD], den[:, i].unsqueeze(2).to_broadcast([P, HEADS, HD]),
                                       ALU.mult)

            def divide_and_sum(c, u):
                done.sync()
                src = qkv[(u - 1) % 2]
                wait(dve, share_done, 3 * c + u - 1)
                wait(dve, attnT_psum, KC * c)
                first = divide_1(src)
                kv_sums(0)
                second = divide_2(first)
                kv_sums(1)
                done.later(divide_3(second, c, u - 2, src))

            def residual_1(c):
                wait(dve, a_ready, TPB * c)
                wait(dve, wo_psum, c)
                flat = xmid[:].rearrange("p t d -> p (t d)")
                for k, bnk in enumerate((p_b2, p_b3)):
                    done.later(v.tensor_tensor(flat[:, 512 * k:512 * k + 512],
                                               flat[:, 512 * k:512 * k + 512], bnk[:], ALU.add))
                done.sync()
                stats(lambda t: xmid[:, t, :], mv_b)
                v.tensor_scalar(sq_b[:], mv_b[:, :, 1], 1.0, EPS, ALU.mult, ALU.add).then_inc(ln2_var, 1)

            def residual_2(c):
                wait(dve, xsum_ready, c)
                wait(dve, out_stored, 16 * (c - 1))
                flat, res = (z[:].rearrange("p t d -> p (t d)") for z in (x1, xres))
                for k, bnk in enumerate((p_b0, p_b1)):
                    wait(dve, proj_psum, 2 * (c - 1) + k + 1)
                    done(v.tensor_tensor(flat[:, 512 * k:512 * k + 512],
                                         res[:, 512 * k:512 * k + 512], bnk[:], ALU.add))
                    for t in range(TPB // 2 * k, TPB // 2 * (k + 1)):
                        done.later(v.bn_stats(st6[:, t, :], x1[:, t, :]))
                averages(mv_b)
                v.tensor_scalar(sq_b[:], mv_b[:, :, 1], 1.0, EPS, ALU.mult, ALU.add).then_inc(x1_read, 1)

            def choose(c):
                wait(dve, logits_psum, c)
                stand_alone(dve)
                logit = [p_b1[:, LOGITS + t * EXPERTS:LOGITS + (t + 1) * EXPERTS] for t in range(TPB)]
                for t in range(TPB):
                    done.later(v.max(top_v[:, t, :], logit[t]))
                done.sync()
                stand_alone(dve)
                for t in range(TPB):
                    done.later(v.max_index(top_i[:, t, :], top_v[:, t, :], logit[t]))
                v.tensor_tensor(gap[:], top_v[:, :, 1], top_v[:, :, 0], ALU.subtract).then_inc(gap_ready, 1)
                wait(dve, scattered, 16 * 2 * TPB * (c - 1))
                done.sync()
                done(v.tensor_copy(first2[:], top_i[:, :, 0:2].rearrange("p t s -> p s t")))
                for s in range(2):
                    done.later(v.tensor_tensor(
                        onehot[:, s], iota_e[:].unsqueeze(1).to_broadcast([P, TPB, EXPERTS]),
                        first2[:, s, :].unsqueeze(2).to_broadcast([P, TPB, EXPERTS]), ALU.is_equal))
                done.sync()
                v.tensor_tensor(chosen[:], onehot[:, 0], onehot[:, 1], ALU.add).then_inc(chosen_ready, 1)

            def place(c):
                n = TPB * EXPERTS
                wait(dve, ranks_psum, c)
                done.later(v.tensor_tensor(
                    rank[:], p_b1[:, RANKS:RANKS + n].rearrange("p (t e) -> p t e", t=TPB),
                    free_row[:].unsqueeze(1).to_broadcast([P, TPB, EXPERTS]), ALU.add))
                done.sync()
                done.later(v.tensor_tensor(
                    slot_w[:].rearrange("p s t e -> p s (t e)"),
                    onehot[:].rearrange("p s t e -> p s (t e)"),
                    rank[:].rearrange("p t e -> p (t e)").unsqueeze(1).to_broadcast([P, 2, n]), ALU.mult))
                v.tensor_tensor(free_row[:], free_row[:], p_b1[:, RANKS + n:RANKS + n + EXPERTS],
                                              ALU.add).then_inc(ranks_read, 1)
                done.sync()
                with nc.allow_low_precision(reason="row numbers are whole and below 2^24"):
                    done.later(v.tensor_reduce(slot[:], slot_w[:].rearrange("p s t e -> p (s t) e"),
                                               AX.X, ALU.add))

            def weights(c):
                wait(dve, gap_exp, c)
                done(v.tensor_scalar(gap[:], gap_e[:], 1.0, None, ALU.add))
                done(v.reciprocal(rows[:, :, C_W0], gap[:]))
                v.tensor_tensor(rows[:, :, C_W1], gap_e[:], rows[:, :, C_W0], ALU.mult).then_inc(slots_ready, 1)

            def finish(c):
                wait(dve, down_psum, c - 1)
                flat = x1[:].rearrange("p t d -> p (t d)")
                done.later(v.tensor_tensor(flat[:, 0:512], flat[:, 0:512], p_b0[:], ALU.add))
                v.tensor_tensor(flat[:, 512:1024], flat[:, 512:1024], p_b1[:], ALU.add).then_inc(out_ready, 1)

            def body(c, core, stage_b, tail):
                last = isinstance(c, int) and c >= BLOCKS - 1
                if core:
                    features(c, 1)
                    kv_products(1)
                    done.sync()
                    kv_sums(0)
                if stage_b:
                    residual_1(c)
                if core:
                    keep_scales(c)
                if stage_b:
                    scales_b(ln2_std, ln2_scale, c)
                if core:
                    if not last:
                        ln1_stats(c + 1)
                    kv_sums(1)
                    share(c, 1)
                    q_products(1)
                    if not last:
                        ln1_scales(c + 1)
                    q_sums(1)
                    features(c, 2)
                    kv_products(2)
                if tail:
                    finish(c)
                if core:
                    divide_and_sum(c, 2)
                    share(c, 2)
                    q_products(2)
                    q_sums(2)
                    features(c, 3)
                    kv_products(3)
                if stage_b:
                    residual_2(c)
                    scales_b(ln3_std, ln3_scale, c)
                if core:
                    divide_and_sum(c, 3)
                    share(c, 3)
                    q_products(3)
                if stage_b:
                    choose(c)
                if core:
                    if not last:
                        wait(dve, pool_qkv, c + 1)
                        features(c + 1, 0)
                    q_sums(3)
                    wait(dve, attnT_psum, KC * c)
                    wait(dve, pool_qkv, c + 1)
                    wait(dve, share_done, 3 * c + 3)
                    done.sync()
                    ones = [divide_1(src, i) for i, src in enumerate((qkv_pool, qkv[1]))]
                    twos = [divide_2(first, i) for i, first in enumerate(ones)]
                    done.later(divide_3(twos[0], c, POOL_TILE, qkv_pool, 0))
                    divide_3(twos[1], c, 2, qkv[1], 1).then_inc(attn_ready, 1)
                if stage_b:
                    place(c)
                    weights(c)

            dve.wait_ge(pool_const, 4)
            ln1_stats(0)
            announce(dve, v.memset(act_tmp[:], 0.0), tmp_ready, 1)
            ln1_scales(0)

            dve.wait_ge(weights_in[0], 16 * 7)
            dve.wait_ge(pool_const, 6)
            done(v.memset(bias_bf[:], 0.0))
            for lo, hi in ((0, 3 * D), (3 * D, 5 * D)):
                left, part, high = prod[:, lo:hi], prod[:, 5 * D + lo:5 * D + hi], bias_hi[:, lo:hi]
                for row in (0, 32, 64):
                    ins = v.tensor_copy(bias_bf[row:row + 1, lo:hi], left[row:row + 1, :])
                    if row < 64:
                        done(ins)
                        done(v.tensor_copy(high, left))
                        done(v.tensor_copy(part, high))
                        done(v.tensor_tensor(left, left, part, ALU.subtract))
                if lo == 0:
                    announce(dve, ins, bias_ready, 1)
                else:
                    done(ins)
            done(v.tensor_copy(free_row[:], iota_r[:]))
            done(v.memset(pad_row[:, D:ROW], 0.0))
            done(v.tensor_scalar(pad_row[:, C_TOK:C_TOK + 1], iota_p[:], float(TOKENS), None, ALU.add))
            v.memset(pad_row[:, 0:D], 0.0).then_inc(const_ready, 1)
            features(0, 0)

            for c in range(FIRST):
                body(c, True, c >= 1, c >= 2)
            with dve.Fori(FIRST, LAST - 1) as c:
                done.enter(c - FIRST, DVE_STEPS)
                body(c, True, True, True)
                done.leave(LAST - 1 - FIRST)
            body(BLOCKS - 1, True, True, True)
            body(BLOCKS, False, True, True)

            announce(dve, v.tensor_scalar(pad_at[:], free_row[:], iota_p[:, 0:1], None, ALU.add), pads_at, 1)
            done(v.tensor_tensor(tiles_f, free_row[:], iota_r[:], ALU.subtract))
            done(v.tensor_scalar(cnt_i, tiles_f, float(P - 1), None, ALU.add))
            done(v.tensor_scalar(cnt_i, cnt_i, P.bit_length() - 1, None, ALU.arith_shift_right))
            done(v.tensor_copy(tiles_f, cnt_i))
            done(v.tensor_copy(tiles_to, tiles_f))
            for e in range(1, EXPERTS):
                done(v.tensor_tensor(tiles_to[:, e:e + 1], tiles_to[:, e:e + 1], tiles_to[:, e - 1:e], ALU.add))
            over = prod[:, 0:SORTED_TILES * EXPERTS].rearrange("p (k e) -> p k e", e=EXPERTS)
            wide = [P, SORTED_TILES, EXPERTS]
            dve.wait_ge(pool_const, 7)
            done(v.tensor_tensor(over, iota_k.unsqueeze(2).to_broadcast(wide),
                                 tiles_to.unsqueeze(1).to_broadcast(wide), ALU.is_ge))
            done(v.tensor_reduce(tab_e, over, AX.X, ALU.add))
            done(v.tensor_scalar(tab_ei, tab_e, float(EXPERTS - 1), None, ALU.min))
            done(v.tensor_tensor(over, over, tiles_f.unsqueeze(1).to_broadcast(wide), ALU.mult))
            done(v.tensor_reduce(tab_first, over, AX.X, ALU.add))
            done(v.tensor_tensor(tab_first, iota_k, tab_first, ALU.subtract))
            done(v.tensor_scalar(tab_first, tab_first, float(P), None, ALU.mult))
            v.scalar_tensor_tensor(tab_row, tab_e, float(REGION), tab_first, ALU.mult, ALU.add
                                   ).then_inc(tables_ready, 1)
            wait(dve, up_taken, 2 * HCH * BLOCKS)
            announce(dve, v.tensor_tensor(sg_g, sg_g, sg_u, ALU.mult), shared_h, BLOCKS)
            body(BLOCKS + 1, False, False, True)

            def keep_meta(k, j):
                dve.wait_ge(xg_loaded[j], 16 * (k // 2 + 1) if isinstance(k, int) else 8 * (k - j) + 16)
                announce(dve, v.tensor_copy(meta, xg[j][:, D:ROW]), xg_meta, k + 1)

            def meta_weights(k, j):
                wait(dve, added, 16 * (k - 1))
                tok_c, w0, w1, e0 = (meta[:, i - D:i - D + 1] for i in (C_TOK, C_W0, C_W1, C_E0))
                done.later(v.tensor_copy(tok_i[j], tok_c))
                done(v.tensor_tensor(w_tmp[:, 0:1], e0, tab_e[:, bass.ds(k, 1)], ALU.is_equal))
                done(v.scalar_tensor_tensor(w_tmp[:, 1:2], w_tmp[:, 0:1], 0.0, w1, ALU.is_equal, ALU.mult))
                announce(dve, v.scalar_tensor_tensor(w_row[j], w0, w_tmp[:, 0:1], w_tmp[:, 1:2],
                                                     ALU.mult, ALU.add), w_ready, k + 1)

            def gated(k, j):
                dve.wait_ge(g_act, k + 1)
                dve.wait_ge(gu_psum, k + 1)
                wait(dve, hgT_psum, k)
                announce(dve, v.tensor_tensor(hg, hact, up_bank[j][:, 0:HALF], ALU.mult), hg_ready, k + 1)

            def take_hT(k, j):
                dve.wait_ge(hgT_psum, k + 1)
                wait(dve, y_psum, k - 1)
                announce(dve, v.tensor_copy(hgT[j], p_core[:, 0:HALF]), hgT_ready, k + 1)

            def tile(k, j):
                keep_meta(k, j)
                gated(k, j)
                take_hT(k, j)
                meta_weights(k, j)
            tile(0, 0)
            tile(1, 1)
            with dve.Fori(1, SORTED_TILES // 2) as m:
                done.enter(m - 1, 6)
                tile(2 * m, 0)
                tile(2 * m + 1, 1)
                done.leave(SORTED_TILES // 2 - 1)
            tile(SORTED_TILES - 1, 0)

        @block.tensor
        def _(pe):
            t_ = nc.tensor

            def project_x(c, u, part):
                n = 4 * c + u
                if part == "T":
                    wait(pe, xhat_ready, TPB * (c + 1))
                    wait(pe, xnT_ready, n)
                    for k in range(KC):
                        ins = t_.transpose(p_xT[:, k * P:(k + 1) * P],
                                           xin[:, ORDER[u], k * P:(k + 1) * P], ident[:])
                    ins.then_inc(xT_psum, 1)
                else:
                    wait(pe, xnT_ready, n + 1)
                    wait(pe, qkv_taken, n)
                    parts = ((p_q0, 0, 512), (p_q1, 512, 768))
                    for bnk, lo, hi in parts:
                        for k in range(KC):
                            t_.matmul(bnk[:, 0:hi - lo], xnT[u % 2][:, k, :], wqkv_sb[:, k, lo:hi],
                                      start=k == 0, stop=False)
                    if isinstance(n, int) and n == 0:
                        pe.wait_ge(bias_ready, 1)
                    for bnk, lo, hi in parts:
                        ins = t_.matmul(bnk[:, 0:hi - lo], ones_bf[:], bias_bf[:, lo:hi],
                                        start=False, stop=True)
                    ins.then_inc(qkv_psum, 1)

            def transpose_block(src, banks, ready, tile_ready=None):
                for t in range(TPB):
                    if tile_ready:
                        tile_ready(t)
                    for k, bnk in enumerate(banks):
                        ins = t_.transpose(bnk[:, t * P:(t + 1) * P], src[:, t, k * P:(k + 1) * P], ident[:])
                        if t == TPB - 1:
                            ins.then_inc(ready, 1)

            def to_tokens(src, chunks, w, banks, bias_at, ready, at_last_chunk=None, between=None,
                          per_bank=False):
                for t in range(TPB):
                    o = banks[t // 2][:, (t % 2) * D:(t % 2 + 1) * D]
                    if t >= 2 and between:
                        between(t - 2)
                    for k in range(chunks):
                        if t == 0 and k == chunks - 1 and at_last_chunk:
                            at_last_chunk()
                        ins = t_.matmul(o, src[:, k, t * P:(t + 1) * P], w[:, k, :], start=k == 0,
                                        stop=bias_at is None and k == chunks - 1)
                    if bias_at is not None:
                        ins = t_.matmul(o, ones_bf[:], bias_bf[:, bias_at:bias_at + D], start=False, stop=True)
                    if t % 2 == 1 and (t == TPB - 1 or per_bank):
                        ins.then_inc(ready, 1)

            def body(c, core, stage_b, tail):
                more = core and (not isinstance(c, int) or c < BLOCKS - 1)
                if core:
                    project_x(c, 2, "T")
                if stage_b:
                    wait(pe, attn_ready, c)
                    wait(pe, ranks_read, c - 1)
                    wait(pe, up_taken, 2 * HCH * (c - 1) - 2)
                    transpose_block(attn, (p_b0, p_b1), attnT_psum)
                if core:
                    project_x(c, 3, "T")
                if stage_b:
                    if isinstance(c, int) and c == 1:
                        pe.wait_ge(const_ready, 1)
                        pe.wait_ge(weights_in[1], 16 * 3)
                        pe.wait_ge(weights_in[2], 16 * 3)
                    wait(pe, up_taken, 2 * HCH * (c - 1))
                    wait(pe, attnT_ready, KC * (c - 1) + 1)
                    to_tokens(bT, KC, wo_sb, (p_b2, p_b3), 3 * D, wo_psum,
                              at_last_chunk=lambda: wait(pe, attnT_ready, KC * c))
                if core:
                    project_x(c, 2, "P")
                if tail:
                    wait(pe, shared_h, c - 1)
                    if not stage_b:
                        wait(pe, ranks_read, c - 1)
                    to_tokens(sg_g, HCH, sgdn_sb, (p_b0, p_b1), None, down_psum)
                if stage_b:
                    transpose_block(hnorm, (p_b2, p_b3), hT_psum,
                                    lambda t: wait(pe, h_ready, TPB * (c - 1) + t + 1))
                if core:
                    project_x(c, 3, "P")
                if stage_b:
                    wait(pe, hT_ready, KC * (c - 1) + 1)
                    for f in range(FCH):
                        if f >= 2:
                            wait(pe, gelu_ready, FCH * (c - 1) + f - 1)
                        bnk = (p_b2, p_b3)[f % 2]
                        for k in range(KC):
                            if f == 0 and k == KC - 1:
                                wait(pe, hT_ready, KC * c)
                            ins = t_.matmul(bnk[:], fc_sb[:, k, f * P:(f + 1) * P], bT[:, k, :],
                                            start=k == 0, stop=k == KC - 1)
                        ins.then_inc(fc_psum, 1)
                    wait(pe, gelu_ready, FCH * c - 1)
                    wait(pe, out_ready, c - 1)
                    to_tokens(hid, FCH, proj_sb, (p_b0, p_b1), 4 * D, proj_psum,
                              at_last_chunk=lambda: wait(pe, gelu_ready, FCH * c),
                              between=(lambda u: project_x(c + 1, u, "T")) if more else None,
                              per_bank=True)
                elif more:
                    project_x(c + 1, 0, "T")
                    project_x(c + 1, 1, "T")
                if more:
                    project_x(c + 1, 0, "P")
                    project_x(c + 1, 1, "P")
                if stage_b:
                    transpose_block(rows, (p_b2, p_b3), x3T_psum,
                                    lambda t: wait(pe, rows_ready, TPB * (c - 1) + t + 1))
                    wait(pe, x3T_ready, KC * c)
                    for t in range(TPB):
                        for k in range(KC):
                            at = LOGITS + t * EXPERTS
                            ins = t_.matmul(p_b1[:, at:at + EXPERTS], bT[:, k, t * P:(t + 1) * P],
                                            gate_sb[:, k, :], start=k == 0, stop=k == KC - 1)
                    ins.then_inc(logits_psum, 1)
                    for n in range(2 * HCH):
                        if n >= 3:
                            wait(pe, up_taken, 2 * HCH * (c - 1) + n - 2)
                        lo = (n % 2) * HALF + (n // 2) * P
                        for k in range(KC):
                            ins = t_.matmul(shared_bank[n % 3][:], sgup_sb[:, k, lo:lo + P], bT[:, k, :],
                                            start=k == 0, stop=k == KC - 1)
                        ins.then_inc(up_psum, 1)
                        if n == 2:
                            ranks(c)

            def ranks(c):
                wait(pe, chosen_ready, c)
                for t in range(TPB + 1):
                    o = p_b1[:, RANKS + t * EXPERTS:RANKS + (t + 1) * EXPERTS]
                    for s in range(t):
                        ins = t_.matmul(o, ones_bf[:], chosen[:, s, :], start=s == 0, stop=s == TPB - 1)
                    if t < TPB:
                        t_.matmul(o, before_bf[:], chosen[:, t, :], start=t == 0, stop=True)
                ins.then_inc(ranks_psum, 1)

            pe.wait_ge(pool_const, 6)
            pe.wait_ge(weights_in[0], 16 * 7)
            project_x(0, 0, "T")
            project_x(0, 1, "T")
            project_x(0, 0, "P")
            project_x(0, 1, "P")
            for c in range(FIRST):
                body(c, True, c >= 1, c >= 2)
            with pe.Fori(FIRST, LAST - 1) as c:
                body(c, True, True, True)
            body(BLOCKS - 1, True, True, True)
            body(BLOCKS, False, True, True)
            body(BLOCKS + 1, False, False, True)

            def expert(k):
                return pe.value_load(tab_ei[0:1, bass.ds(k, 1)], min_val=0, max_val=EXPERTS - 1)

            def exp_w(e, lo, hi):
                return exp_sb[:, bass.ds(e, 1), lo:hi].rearrange("p a n -> p (a n)")

            def gT(k, j):
                pe.wait_ge(xg_loaded[j], 16 * (k // 2 + 1) if isinstance(k, int) else 8 * (k - j) + 16)
                wait(pe, gT_ready, k)
                for c in range(KC):
                    ins = t_.transpose(p_xT[:, c * P:(c + 1) * P], xg[j][:, c * P:(c + 1) * P], ident[:])
                ins.then_inc(gT_psum, 1)

            def gate_up(k, j, e):
                pe.wait_ge(gT_ready, k + 1)
                wait(pe, hg_ready, k - 1)
                for bnk, lo, ready in ((gate_bank[j], 0, gate_psum), (up_bank[j], HALF, gu_psum)):
                    for c in range(KC):
                        at = c * 2 * HALF + lo
                        ins = t_.matmul(bnk[:, 0:HALF], xgT[j][:, c * P:(c + 1) * P],
                                        exp_w(e, at, at + HALF), start=c == 0, stop=c == KC - 1)
                    ins.then_inc(ready, 1)

            def hT(k, j):
                pe.wait_ge(hg_ready, k + 1)
                wait(pe, hgT_ready, k)
                for c in range(HCH):
                    ins = t_.transpose(p_core[:, c * P:(c + 1) * P], hg[:, c * P:(c + 1) * P], ident[:])
                ins.then_inc(hgT_psum, 1)

            def down(k, j, e):
                pe.wait_ge(hgT_ready, k + 1)
                wait(pe, y_ready, k - 1)
                for c in range(HCH):
                    at = KC * 2 * HALF + c * D
                    ins = t_.matmul(y_bank[j][:, 0:D], hgT[j][:, c * P:(c + 1) * P], exp_w(e, at, at + D),
                                    start=c == 0, stop=c == HCH - 1)
                ins.then_inc(y_psum, 1)

            pe.wait_ge(tables_ready, 1)
            pe.wait_ge(experts_in, 16 * EXPERTS)
            gT(0, 0)
            gate_up(0, 0, expert(0))
            gT(1, 1)
            hT(0, 0)
            gate_up(1, 1, expert(1))

            def step(k, j):
                gT(k + 1, 1 - j)
                down(k - 1, 1 - j, expert(k - 1))
                e = expert(k + 1)
                hT(k, j)
                gate_up(k + 1, 1 - j, e)
            step(1, 1)
            step(2, 0)
            with pe.Fori(1, (SORTED_TILES - 3) // 2) as m:
                step(2 * m + 1, 1)
                step(2 * m + 2, 0)
            step(SORTED_TILES - 2, 1)
            k = SORTED_TILES - 1
            down(k - 1, 1, expert(k - 1))
            hT(k, 0)
            down(k, 0, expert(k))


def kernel(**inputs):
    import numpy as np
    import concourse.bacc as bacc
    from concourse.bass_utils import run_bass_kernel_spmd

    def get(name):
        return np.asarray(inputs["L0_" + name])

    def rows_of(w):
        return w.reshape(-1, P, w.shape[-1]).transpose(1, 0, 2)

    w_up, w_down = get("ffn_w_up"), get("ffn_w_down")
    experts = np.concatenate([
        w_up.transpose(0, 2, 1).reshape(EXPERTS, KC, P, 2 * HALF).transpose(0, 2, 1, 3).reshape(EXPERTS, P, -1),
        w_down.transpose(0, 2, 1).reshape(EXPERTS, HCH, P, D).transpose(0, 2, 1, 3).reshape(EXPERTS, P, -1),
    ], axis=2)
    arrays = {
        "x": get("attn_q_x").reshape(TOKENS, D),
        "wqkv": rows_of(np.concatenate([get("attn_wq"), get("attn_wk"), get("attn_wv")], axis=1)),
        "b_tok": np.concatenate([get(f"attn_{n}") for n in ("bq", "bk", "bv", "bo", "proj_b")])[None],
        "ln1w": get("attn_ln1_w").reshape(KC, P).T,
        "ln1b": get("attn_ln1_b").reshape(KC, P).T,
        "ln2w": get("attn_ln2_w").reshape(KC, P).T,
        "ln2b": get("attn_ln2_b").reshape(KC, P).T,
        "wo": rows_of(get("attn_wo")),
        "fc_w": rows_of(get("attn_fc_w")),
        "fc_b": get("attn_fc_b").reshape(FCH, P).T,
        "proj_w": rows_of(get("attn_proj_w")),
        "gate_w": rows_of(get("ffn_gate_w").T),
        "sg_up": rows_of(np.concatenate([get("ffn_sg_gate"), get("ffn_sg_up")], axis=0).T),
        "sg_down": rows_of(get("ffn_sg_down").T),
        "experts": experts,
    }
    nc = bacc.Bacc("TRN2", target_bir_lowering=False, num_devices=1)
    feeds, args = {}, []
    for name, a in arrays.items():
        feeds[f"in_{name}"] = np.ascontiguousarray(a)
        args.append(nc.dram_tensor(f"in_{name}", list(a.shape), mybir.dt.from_np(a.dtype),
                                   kind="ExternalInput").ap())
    args.append(nc.dram_tensor("out_rows", [TOKENS + P, D], FP32, kind="ExternalOutput").ap())
    build(nc, *args)
    result = run_bass_kernel_spmd(nc, [feeds], core_ids=[0]).results[0]
    return result["out_rows"][0:TOKENS].reshape(16, 512, D)
```
